# Optimizing a Trainium2 kernel written in Bass

```python
import numpy as np
import jax
import jax.numpy as jnp

def _softmax(x, axis=-1):
    return jax.nn.softmax(x, axis=axis)

def _gelu(x):
    return jax.nn.gelu(x, approximate=True)

def _silu(x):
    return jax.nn.silu(x)

def _sigmoid(x):
    return jax.nn.sigmoid(x)

def _layernorm(x, axis=-1, eps=1e-05):
    m = jnp.mean(x, axis=axis, keepdims=True)
    v = jnp.var(x, axis=axis, keepdims=True)
    return (x - m) / jnp.sqrt(v + eps)

def _scatter_add(tgt, idx, src, axis=0):
    return tgt.at[idx].add(src)

def _segment_sum(src, seg, n):
    return jax.ops.segment_sum(src, seg, n)
kernel_name = 'mk_flamingo_gated_d1_seqx_r4_55e778'

def setup_inputs(seed: int=0):
    np.random.seed(seed)
    _w = jnp.asarray

    def _rec_inputs():
        import jax
        import jax.numpy as jnp
        _rk = jax.random.key(seed)
        x = -0.000125 + 0.9999 * jax.random.normal(jax.random.fold_in(_rk, 1), (4, 512, 512), jnp.float32)
        _lenS = 512 - jax.random.randint(jax.random.fold_in(_rk, 7), (4,), 0, max(1, 512 // 4) + 1, jnp.int32)
        _lenS2 = 512 - jax.random.randint(jax.random.fold_in(_rk, 8), (4,), 0, max(1, 512 // 4) + 1, jnp.int32)
        itok_BxS_13_99985 = jax.random.randint(jax.random.fold_in(_rk, 11), (4, 512), 13, 99986, jnp.int32)
        _ctx_2048P = jax.random.normal(jax.random.fold_in(_rk, 12), (4, 16, 512), jnp.float32)
        _ctx_2048c = jax.random.dirichlet(jax.random.fold_in(_rk, 512), 0.3 * jnp.ones((16,), jnp.float32), (4, 512))
        _ctx_2048t = jnp.einsum('bsk,bkd->bsd', _ctx_2048c, _ctx_2048P)
        _ctx_2048t = _ctx_2048t * jax.lax.rsqrt(jnp.mean(jnp.square(_ctx_2048t)) + 1e-12) * 0.953939
        ctx_2048 = 6.82029e-06 + 0.0200006 * (_ctx_2048t + 0.3 * jax.random.normal(jax.random.fold_in(_rk, 612), (4, 512, 512), jnp.float32))
        _g = jax.random.normal(jax.random.fold_in(_rk, 9001), (2, 1), jnp.float32)
        _g = jnp.sign(_g) * jnp.maximum(jnp.abs(_g), 1.0) + (_g == 0) * 1.0
        g_xattn = _g[0]
        g_ffn = _g[1]
        return (x, itok_BxS_13_99985, ctx_2048, g_xattn, g_ffn)
    x, itok_BxS_13_99985, ctx_2048, g_xattn, g_ffn = _rec_inputs()

    def _L0_xattn_setup():
        import jax, jax.numpy as jnp
        import numpy as np
        B, S, D = (4, 1024, 512)
        E = 4
        F = 2048 // E
        VOCAB = 25000
        key = jax.random.key(seed)
        k1, k2, k3, k4, k5 = jax.random.split(key, 5)
        hidden_states = jax.random.normal(k1, (B, S, D), dtype=jnp.float32)
        token_ids = jax.random.randint(k2, (B, S), 0, VOCAB, dtype=jnp.int64)
        Wg = jax.random.normal(k3, (E, F, D), dtype=jnp.float32) * 0.02
        Wu = jax.random.normal(k4, (E, F, D), dtype=jnp.float32) * 0.02
        Wd = jax.random.normal(k5, (E, D, F), dtype=jnp.float32) * 0.02
        return {'hidden_states': hidden_states, 'token_ids': token_ids, 'Wg': Wg, 'Wu': Wu, 'Wd': Wd}
    _L0_xattn_all = _L0_xattn_setup()
    _L0_xattn_in = {k: v for k, v in _L0_xattn_all.items() if k in ()}
    del _L0_xattn_all

    def _L0_ffn_setup():
        import jax, jax.numpy as jnp
        import numpy as np
        HIDDEN = 512
        INTER = 1408
        B, S = (2, 512)

        def _ternary(key, shape):
            return jax.random.randint(key, shape, -1, 2).astype(jnp.float32)
        key = jax.random.key(seed)
        ks = jax.random.split(key, 7)
        x = jax.random.normal(ks[0], (B, S, HIDDEN), dtype=jnp.float32)
        gate_w = _ternary(ks[1], (INTER, HIDDEN))
        up_w = _ternary(ks[2], (INTER, HIDDEN))
        down_w = _ternary(ks[3], (HIDDEN, INTER))
        gate_s = jax.random.uniform(ks[4], (INTER,), minval=0.01, maxval=0.1, dtype=jnp.float32)
        up_s = jax.random.uniform(ks[5], (INTER,), minval=0.01, maxval=0.1, dtype=jnp.float32)
        down_s = jax.random.uniform(ks[6], (HIDDEN,), minval=0.01, maxval=0.1, dtype=jnp.float32)
        return {'x': x, 'gate_w': gate_w, 'up_w': up_w, 'down_w': down_w, 'gate_s': gate_s, 'up_s': up_s, 'down_s': down_s}
    _L0_ffn_all = _L0_ffn_setup()
    _L0_ffn_in = {k: v for k, v in _L0_ffn_all.items() if k in ('gate_w', 'up_w', 'down_w', 'gate_s', 'up_s', 'down_s')}
    del _L0_ffn_all
    return {'x': x, 'itok_BxS_13_99985': itok_BxS_13_99985, 'ctx_2048': ctx_2048, 'g_xattn': g_xattn, 'g_ffn': g_ffn, 'L0_ffn_gate_w': _L0_ffn_in['gate_w'], 'L0_ffn_up_w': _L0_ffn_in['up_w'], 'L0_ffn_down_w': _L0_ffn_in['down_w'], 'L0_ffn_gate_s': _L0_ffn_in['gate_s'], 'L0_ffn_up_s': _L0_ffn_in['up_s'], 'L0_ffn_down_s': _L0_ffn_in['down_s']}

def reference(x, itok_BxS_13_99985, ctx_2048, g_xattn, g_ffn, L0_ffn_gate_w, L0_ffn_up_w, L0_ffn_down_w, L0_ffn_gate_s, L0_ffn_up_s, L0_ffn_down_s):
    import jax
    import jax.numpy as jnp

    def _L0_xattn_ref(hidden_states, token_ids, Wg, Wu, Wd):
        import jax, jax.numpy as jnp
        import numpy as np
        B, S, D = (4, 1024, 512)
        E = 4
        F = 2048 // E
        VOCAB = 25000
        tokens_per_expert = VOCAB // E
        tid = jnp.clip(token_ids, 0, VOCAB - 1)
        expert_ids = jnp.minimum(tid // tokens_per_expert, E - 1)
        out = jnp.zeros_like(hidden_states)
        for e in range(E):
            g = jax.nn.silu(jnp.einsum('bsd,fd->bsf', hidden_states, Wg[e]))
            u = jnp.einsum('bsd,fd->bsf', hidden_states, Wu[e])
            y = jnp.einsum('bsf,df->bsd', g * u, Wd[e])
            out = jnp.where((expert_ids == e)[..., None], y, out)
        return out

    def _L0_ffn_ref(x, gate_w, up_w, down_w, gate_s, up_s, down_s):
        import jax, jax.numpy as jnp
        import numpy as np
        HIDDEN = 512
        INTER = 1408
        B, S = (2, 512)

        def _ternary(key, shape):
            return jax.random.randint(key, shape, -1, 2).astype(jnp.float32)
        b, s, h = x.shape
        xf = x.reshape(b * s, h)
        g = jnp.einsum('th,ih->ti', xf, gate_w) * gate_s
        u = jnp.einsum('th,ih->ti', xf, up_w) * up_s
        hdn = jax.nn.silu(g) * u
        out = jnp.einsum('ti,hi->th', hdn, down_w) * down_s
        return out.reshape(b, s, -1)
    x = x + jnp.tanh(g_xattn[0]) * _L0_xattn_ref(_layernorm(x, axis=-1), itok_BxS_13_99985, ctx_2048, ctx_2048, ctx_2048)
    x = x + jnp.tanh(g_ffn[0]) * _L0_ffn_ref(_layernorm(x, axis=-1), L0_ffn_gate_w, L0_ffn_up_w, L0_ffn_down_w, L0_ffn_gate_s, L0_ffn_up_s, L0_ffn_down_s)
    return x

_drawn_inputs = setup_inputs


def setup_inputs(seed=0):
    import zlib

    import numpy as np

    out = dict(_drawn_inputs(seed))
    spreads = {}
    factors = {}
    for name, (base, spread) in spreads.items():
        noise = np.random.default_rng([zlib.crc32(name.encode()), seed]).standard_normal(out[name].shape)
        drawn = base * np.exp(spread * noise) if base else spread * noise
        out[name] = jnp.asarray(drawn.astype(out[name].dtype))
    for name, factor in factors.items():
        out[name] = (out[name] * factor).astype(out[name].dtype)
    return out
```

```python
from contextlib import ExitStack

import concourse.bass as bass
from concourse import mybir
from concourse.bass import ds

F32 = mybir.dt.float32
F32R = mybir.dt.float32r
FP16 = mybir.dt.float16
I32 = mybir.dt.int32
U32 = mybir.dt.uint32
ALU = mybir.AluOpType
ACT = mybir.ActivationFunctionType
AX = mybir.AxisListType.X

P = 128
TOKENS = 2048
D = 512
KC = D // P
EXPERTS = 4
VOCAB = 25000
PER_EXPERT = VOCAB // EXPERTS
TILES = TOKENS // P
STEPS = TILES + EXPERTS - 1
CT = TOKENS // P
INTER = 1408
IC = INTER // P
BLOCK = 4
BLOCKS = TILES // BLOCK
PIECE = INTER // 2
PIECES = 2 * KC * 2
RING = 6
ROWS = 8
RAWS = 4
EPS = 1e-5
PASSES = [(0, 0), (1, 0), (0, 1)]
CTX_WORDS = EXPERTS * KC * 2 * D
XBUF_WORDS = BLOCK * 2 * D
PREP_AT = {5: 0, 6: 1, 7: 2, 8: 3}


def ring_slot(k):
    return (k + 4) % RING


def row_slot(b, t):
    return (RING + BLOCK * b + t) % ROWS


def build(nc, x, ids, ctxT, g_x, g_f, guT, dwT, gate_s, up_s, down_s, out):
    scratch = nc.dram_tensor("x1_rows", [2 * TOKENS + STEPS * P, D], F32).ap()
    ctx_v = ctxT.rearrange("e (c p) f -> e p c f", p=P)
    gu_v = guT.rearrange("(r p) (v n) -> p r v n", p=P, v=2)
    dw_v = dwT.rearrange("(c p) h -> c p h", p=P)
    x1_v = scratch[0:TOKENS, :].rearrange("(t p) h -> p t h", p=P)

    with ExitStack() as ctx:
        def sb(name, shape, dt):
            return ctx.enter_context(nc.sbuf_tensor(name, shape, dt))

        def psum(name):
            return ctx.enter_context(nc.psum_tensor(name, [P, D], F32))

        def sem(name):
            return ctx.enter_context(nc.semaphore(name))

        work = sb("work", [P, CTX_WORDS + XBUF_WORDS], F32R)
        wgu_base = nc.sbuf_base
        wgu = sb("wgu", [P, 2 * KC, 2, INTER], F32R)
        raw_base = nc.sbuf_base
        raw = sb("raw", [P, RAWS, PIECE], F32)
        rows = sb("rows", [P, ROWS, D], F32)
        xn = sb("xn", [P, D], F32)
        sh = sb("sh", [P, D], F32)
        tmp = sb("tmp", [P, D], F32)
        dsb = sb("dsb", [P, D], F32)
        ident = sb("ident", [P, P], F32)
        bn = sb("bn", [P, 6], F32)
        mv = sb("mv", [P, 2], F32)
        ve = sb("ve", [P, 1], F32)
        rstd = sb("rstd", [P, 1], F32)
        half = sb("half", [P, 1], F32)
        gs = sb("gs", [P, 2, IC], F32)
        gg = sb("gg", [P, 2], F32)
        tg = sb("tg", [P, 2], F32)
        gidx = sb("gidx", [P, STEPS], U32)
        sidx = sb("sidx", [P, STEPS], U32)
        oidx = sb("oidx", [P, TILES], U32)
        eidx = sb("eidx", [1, STEPS], I32)
        inow = sb("inow", [P, 2], U32)


        hp = nc.alloc_sbuf_tensor_at("hp", [P, 2, 2, D], F32R, offset=raw_base)
        wgu_bytes = 2 * KC * 2 * INTER * 4
        ctx_in_bytes = EXPERTS * KC * D * 4
        ctx_in = nc.alloc_sbuf_tensor_at("ctx_in", [P, EXPERTS, KC, D], F32,
                                         offset=wgu_base + wgu_bytes - ctx_in_bytes)
        route_at = [wgu_base + 3 * 2 * INTER * 4]

        def rt(name, shape, dt):
            count = 1
            for n in shape[1:]:
                count *= n
            at = route_at[0]
            route_at[0] = (at + count * (2 if dt == FP16 else 4) + 31) // 32 * 32
            assert route_at[0] <= wgu_base + wgu_bytes - ctx_in_bytes
            return nc.alloc_sbuf_tensor_at(name, shape, dt, offset=at)

        ids_i = rt("ids_i", [P, CT], I32)
        ids_f = rt("ids_f", [P, CT], F32)
        at_least = rt("at_least", [P, EXPERTS + 1, CT], F32)
        of = rt("of", [P, EXPERTS, CT], F32)
        ones_f = rt("ones_f", [P, EXPERTS * CT], F32)
        seen = rt("seen", [P, EXPERTS, CT], F32)
        here = rt("here", [P, EXPERTS], F32)
        here16 = rt("here16", [P, EXPERTS], FP16)
        tri = rt("tri", [P, P], FP16)
        ones16 = rt("ones16", [P, P], FP16)
        before = rt("before", [P, 2, EXPERTS], F32)
        pad_i = rt("pad_i", [P, EXPERTS], I32)
        pad = rt("pad", [P, EXPERTS], F32)
        pad_end = rt("pad_end", [P, EXPERTS], F32)
        end = rt("end", [P, EXPERTS], F32)
        small = [rt(f"small{n}", [P, EXPERTS], F32) for n in range(6)]
        pos = [rt(f"pos{n}", [P, EXPERTS, CT], F32) for n in range(3)]
        slot = rt("slot", [P, CT], F32)
        shift = rt("shift", [P, CT], F32)
        rank = rt("rank", [P, CT], F32)
        place_i = rt("place_i", [P, 2, CT], I32)
        low_i = rt("low_i", [P, 2, CT], I32)
        high_i = rt("high_i", [P, 2, CT], I32)
        low = rt("low", [P, 2, CT], F32)
        high = rt("high", [P, 2, CT], F32)
        iota_p = rt("iota_p", [P, P], F32)
        token = rt("token", [P, CT], F32)
        dump = rt("dump", [P, STEPS], F32)
        tile_at = rt("tile_at", [1, STEPS], F32)
        is_low = [rt(f"is_low{n}", [P, CT, P], FP16) for n in range(2)]
        is_high = rt("is_high", [P, CT, 3, STEPS], FP16)
        is_high2 = rt("is_high2", [P, CT, TILES], FP16)
        table = rt("table", [P, 3, STEPS], F32)
        empty = rt("empty", [P, 2, STEPS], F32)
        owner = rt("owner", [1, 3, STEPS], F32)

        bank = [psum(f"bank{n}") for n in range(8)]
        z_ps, y_ps, g_ps, u_ps = bank[0], bank[1], bank[0], bank[1]
        acc_ps = bank[2:6]
        xt_ps, ht_ps = bank[6], bank[7]

        def xbuf(b):
            base = CTX_WORDS - XBUF_WORDS * (b % 2)
            return work[:, ds(base, XBUF_WORDS)]

        def xpart(b, u, s):
            base = CTX_WORDS - XBUF_WORDS * (b % 2)
            return work[:, ds(base + (2 * u + s) * D, D)]

        def hpart(s):
            return work[:, CTX_WORDS + (2 + s) * D:CTX_WORDS + (3 + s) * D]

        def ctx_w(e, c, s):
            return work[:, ds(e * (KC * 2 * D) + (c * 2 + s) * D, D)]

        def down_w(c, s):
            return work[:, (c * 2 + s) * D:(c * 2 + s + 1) * D]

        names = """ids_in small_in consts route_pe route_sb route_step tables_ready
            piece_landed piece_hi piece_lo down_hi down_lo x_landed stored rows_a rows_b
            bn_parts bn_mv var_ready rstd_ready xn_ready xt_done xhi_ready xlo_ready
            z_done y_done silu_ready h_ready ht_done hhi_ready hlo_ready u_done d_done rows_ready
            scaled gates_ready dsb_ready ctx_hi ctx_lo out_stored index_now held""".split()
        S = {n: sem(n) for n in names}
        ctx_landed = [sem(f"ctx_landed{e}") for e in range(EXPERTS)]
        down_landed = [sem(f"down_landed{n}") for n in range(4)]
        last_stored = [sem(f"last_stored{t}") for t in range(BLOCK)]

        def hold(eng):
            eng.sem_inc(S["held"])

        block = ctx.enter_context(nc.Block())

        @block.sync
        def _(sp):
            sp.dma_start(ids_i[:, :], ids).then_inc(S["ids_in"], 16)
            for e in range(EXPERTS):
                sp.dma_start(ctx_in[:, e], ctx_v[e]).then_inc(ctx_landed[e], 16)
            for s, src in enumerate((gate_s, up_s)):
                sp.dma_start(gs[:, s, :], src).then_inc(S["small_in"], 16)
            for s, src in enumerate((g_x, g_f)):
                sp.dma_start(gg[:, s:s + 1], src.partition_broadcast(P)).then_inc(S["small_in"], 16)
            sp.dma_start(dsb[:, :], down_s.partition_broadcast(P)).then_inc(S["small_in"], 16)

            def piece_at(q):
                return sp.snap(q % RAWS), sp.snap(q // 2), sp.snap(q % 2), sp.snap(q - RAWS + 1), sp.snap(16 * q)

            def piece(at, row, half_):
                sp.dma_start(raw[:, ds(at, 1), :], gu_v[:, ds(row, 1), ds(half_, 1), :])\
                  .then_inc(S["piece_landed"], 16)

            for q in range(RAWS):
                if q:
                    sp.wait_ge(S["piece_landed"], 16 * q)
                piece(q % RAWS, q // 2, q % 2)
            with sp.Fori(RAWS, PIECES) as q:
                *at, split, all_before = piece_at(q)
                sp.wait_ge(S["piece_landed"], all_before)
                hold(sp)
                sp.wait_ge(S["piece_lo"], split)
                hold(sp)
                piece(*at)

            def load_rows(b):
                for half_, landed in enumerate((S["rows_a"], S["rows_b"])):
                    t = BLOCK * b + 2 * half_
                    at = row_slot(b, 2 * half_)
                    sp.dma_start(rows[:, at:at + 2, :], x1_v[:, t:t + 2, :]).then_inc(landed, 16)
                    if b == 0 and half_ == 0:
                        sp.wait_ge(S["stored"], 16 * 16)

            sp.wait_ge(S["stored"], 16 * (BLOCK + EXPERTS - 1))
            load_rows(0)
            sp.wait_ge(S["stored"], 16 * STEPS)
            for c in range(IC):
                if c >= 4:
                    sp.wait_ge(S["down_lo"], c - 3)
                sp.dma_start(rows[:, 2 + c % 4, :], dw_v[c]).then_inc(down_landed[c % 4], 16)
            sp.wait_ge(S["down_lo"], IC)
            load_rows(1)
            for b in range(2, BLOCKS):
                sp.wait_ge(S["out_stored"], 16 * BLOCK * (b - 1))
                load_rows(b)
            sp.wait_ge(S["out_stored"], 16 * BLOCK * (BLOCKS - 1))
            for t in range(BLOCK):
                sp.wait_ge(last_stored[t], 16)

        @block.gpsimd
        def _(pool):
            pool.memset(half[:, :], -0.5).then_inc(S["consts"], 1)
            pool.memset(ident[:, :], 0.0).then_inc(S["consts"], 1)
            pool.memset(ones16[:, :], 1.0).then_inc(S["consts"], 1)
            pool.wait_ge(S["consts"], 3)
            pool.affine_select(out=ident[:, :], in_=ident[:, :], compare_op=ALU.not_equal, fill=1.0,
                               base=0, pattern=[[-1, P]], channel_multiplier=1).then_inc(S["consts"], 1)
            pool.affine_select(out=tri[:, :], in_=ones16[:, :], compare_op=ALU.is_gt, fill=0.0,
                               base=0, pattern=[[1, P]], channel_multiplier=-1).then_inc(S["consts"], 1)
            exact = dict(allow_small_or_imprecise_dtypes=True)
            pool.iota(iota_p[:, :], pattern=[[1, P]], base=0, channel_multiplier=0, **exact)\
                .then_inc(S["consts"], 1)
            pool.iota(token[:, :], pattern=[[1, CT]], base=0, channel_multiplier=CT, **exact)\
                .then_inc(S["consts"], 1)
            pool.iota(dump[:, :], pattern=[[P, STEPS]], base=TOKENS, channel_multiplier=1, **exact)\
                .then_inc(S["consts"], 1)
            pool.iota(tile_at[:, :], pattern=[[P, STEPS]], base=0, channel_multiplier=0, **exact)\
                .then_inc(S["consts"], 1)
            pool.wait_ge(S["consts"], 9)

            def gather(at, index):
                pool.indirect_dma_start(
                    rows[:, at, :], None, x, bass.IndirectOffsetOnAxis(ap=index, axis=0))\
                    .then_inc(S["x_landed"], 16)

            def store(at, index):
                pool.indirect_dma_start(
                    scratch, bass.IndirectOffsetOnAxis(ap=index, axis=0), rows[:, at, :], None)\
                    .then_inc(S["stored"], 16)

            def inverse_std(m):
                pool.wait_ge(S["var_ready"], m + 1)
                pool.tensor_tensor(rstd[:, :], ve[:, :], half[:, :], ALU.pow)\
                    .then_inc(S["rstd_ready"], 1)

            pool.wait_ge(S["tables_ready"], 1)
            for k in range(5):
                if k:
                    pool.wait_ge(S["x_landed"], 16 * k)
                gather(ring_slot(k), gidx[:, k:k + 1])
                if k >= 1:
                    inverse_std(k - 1) if k <= 2 else None
            inverse_std(2)
            inverse_std(3)
            pool.wait_ge(S["x_landed"], 16 * 5)
            gather(ring_slot(5), gidx[:, 5:6])
            pool.wait_ge(S["rows_ready"], 1)
            store(ring_slot(0), sidx[:, 0:1])

            with pool.Fori(0, 2) as i:
                for j in range(RING):
                    k = 2 + RING * i + j
                    inverse_std(k + 2)
                    pool.wait_ge(S["x_landed"], 16 * (k + 4))
                    pool.tensor_copy(inow[:, 0:1], gidx[:, ds(k + 4, 1)]).then_inc(S["index_now"], 1)
                    pool.wait_ge(S["stored"], 16 * (k - 1))
                    pool.tensor_copy(inow[:, 1:2], sidx[:, ds(k - 1, 1)]).then_inc(S["index_now"], 1)
                    pool.wait_ge(S["index_now"], 2 * (k - 1))
                    hold(pool)
                    gather(ring_slot(2 + j + 4), inow[:, 0:1])
                    pool.wait_ge(S["rows_ready"], k)
                    hold(pool)
                    store(ring_slot(2 + j - 1), inow[:, 1:2])
            for k in range(14, STEPS + 1):
                inverse_std(k + 2)
                if k == STEPS:
                    inverse_std(k + 3)
                if k + 4 < STEPS:
                    pool.wait_ge(S["stored"], 16 * (k - 1))
                    pool.wait_ge(S["x_landed"], 16 * (k + 4))
                    gather(ring_slot(k + 4), gidx[:, k + 4:k + 5])
                pool.wait_ge(S["stored"], 16 * (k - 1))
                pool.wait_ge(S["rows_ready"], k)
                store(ring_slot(k - 1), sidx[:, k - 1:k])

            for b in range(BLOCKS):
                if b + 1 < BLOCKS:
                    for t in range(BLOCK):
                        inverse_std(STEPS + BLOCK * (b + 1) + t)
                for t in range(BLOCK):
                    n = BLOCK * b + t
                    pool.wait_ge(S["rows_ready"], STEPS + n + 1)
                    if b + 1 < BLOCKS:
                        if n:
                            pool.wait_ge(S["out_stored"], 16 * n)
                        done = S["out_stored"]
                    else:
                        done = last_stored[t]
                    pool.indirect_dma_start(
                        out, bass.IndirectOffsetOnAxis(ap=oidx[:, n:n + 1], axis=0),
                        rows[:, row_slot(b, t), :], None).then_inc(done, 16)

        @block.scalar
        def _(act):
            for e in range(EXPERTS):
                act.wait_ge(ctx_landed[e], 16)
                for c in range(KC):
                    act.activation(ctx_w(e, c, 0), ctx_in[:, e, c, :], ACT.Copy).then_inc(S["ctx_hi"], 1)
            act.wait_ge(S["small_in"], 16 * 5)
            act.activation(tg[:, :], gg[:, :], ACT.Tanh).then_inc(S["gates_ready"], 1)

            def x_hi(m, b, u):
                act.wait_ge(S["xt_done"], m + 1)
                act.activation(xpart(b, u, 0), xt_ps[:, :], ACT.Copy).then_inc(S["xhi_ready"], 1)

            def h_hi(k):
                act.wait_ge(S["ht_done"], k + 1)
                act.activation(hpart(0), ht_ps[:, :], ACT.Copy).then_inc(S["hhi_ready"], 1)

            def silu(k):
                act.wait_ge(S["z_done"], k + 1)
                act.activation(sh[:, :], z_ps[:, :], ACT.Silu).then_inc(S["silu_ready"], 1)

            def piece_hi(q):
                act.wait_ge(S["piece_landed"], 16 * (q + 1))
                act.activation(wgu[:, ds(q // 2, 1), 0, ds(q % 2 * PIECE, PIECE)],
                               raw[:, ds(q % RAWS, 1), :], ACT.Copy).then_inc(S["piece_hi"], 1)

            x_hi(0, 0, 0)
            silu(0)
            x_hi(1, 0, 0)
            with act.Fori(1, PIECES + 1) as k:
                h_hi(k - 1)
                piece_hi(k - 1)
                silu(k)
                x_hi(k + 1, 0, 0)
            h_hi(16)
            silu(17)
            x_hi(18, 0, 0)
            h_hi(17)
            x_hi(19, 0, 2)
            silu(18)
            h_hi(18)
            x_hi(20, 0, 3)
            x_hi(21, 0, 0)
            act.wait_ge(S["y_done"], STEPS)
            x_hi(22, 0, 1)

            def down_hi(c):
                act.wait_ge(down_landed[c % 4], 16 * (c // 4 + 1))
                act.activation(down_w(c, 0), rows[:, 2 + c % 4, :], ACT.Copy).then_inc(S["down_hi"], 1)

            def chunk(b, c):
                n = STEPS + IC * b + c
                act.wait_ge(S["z_done"], n + 1)
                act.wait_ge(S["hlo_ready"], n)
                act.activation(sh[:, :], g_ps[:, :], ACT.Silu, scale=gs[:, 0, c:c + 1])\
                   .then_inc(S["silu_ready"], 1)
                act.wait_ge(S["h_ready"], n + 1)
                act.activation(hp[:, n_slot(b, c), 0, :], sh[:, :], ACT.Copy)\
                   .then_inc(S["hhi_ready"], 1)

            for b in range(BLOCKS):
                for c in range(IC):
                    if b == 0:
                        for d in range(3 * c, min(3 * c + 3, IC)):
                            down_hi(d)
                    chunk(b, c)
                    if c in PREP_AT and b + 1 < BLOCKS:
                        t = PREP_AT[c]
                        x_hi(STEPS + BLOCK * (b + 1) + t, b + 1, (t + 2) % BLOCK)

        @block.vector
        def _(dve):
            steps = [0]

            def then(ins):
                steps[0] += 1
                ins.then_inc(S["route_step"], 1)
                dve.wait_ge(S["route_step"], steps[0])

            dve.memset(at_least[:, 0, :], 1.0)
            dve.memset(at_least[:, EXPERTS, :], 0.0)
            dve.memset(ones_f[:, :], 1.0)
            dve.wait_ge(S["ids_in"], 16)
            then(dve.tensor_copy(ids_f[:, :], ids_i[:, :]))
            for e in range(1, EXPERTS):
                ins = dve.tensor_scalar(at_least[:, e, :], ids_f[:, :], float(PER_EXPERT * e), None,
                                        ALU.is_ge)
            then(ins)
            then(dve.tensor_tensor(of[:, :, :], at_least[:, 0:EXPERTS, :], at_least[:, 1:EXPERTS + 1, :],
                                   ALU.subtract))
            dve.tensor_tensor_scan(seen[:, :, :].rearrange("p e c -> p (e c)"), ones_f[:, :],
                                   of[:, :, :].rearrange("p e c -> p (e c)"), 0.0, ALU.mult, ALU.add)
            then(dve.tensor_reduce(here[:, :], of[:, :, :], AX, ALU.add))
            dve.tensor_copy(here16[:, :], here[:, :]).then_inc(S["route_sb"], 1)
            dve.wait_ge(S["route_pe"], 1)
            then(dve.tensor_copy(before[:, :, :].rearrange("p a e -> p (a e)"), bank[2][:, 0:2 * EXPERTS]))
            then(dve.tensor_scalar(pad_i[:, :], before[:, 1, :], float(P - 1), None, ALU.add))
            then(dve.tensor_scalar(pad_i[:, :], pad_i[:, :], -P, None, ALU.bitwise_and))
            then(dve.tensor_copy(pad[:, :], pad_i[:, :]))
            dve.tensor_tensor_scan(pad_end[:, :], ones_f[:, 0:EXPERTS], pad[:, :], 0.0, ALU.mult, ALU.add)
            then(dve.tensor_tensor_scan(end[:, :], ones_f[:, 0:EXPERTS], before[:, 1, :], 0.0,
                                        ALU.mult, ALU.add))
            pad_start, start, offset, prior, first, gap = small
            dve.tensor_tensor(pad_start[:, :], pad_end[:, :], pad[:, :], ALU.subtract)
            dve.tensor_tensor(start[:, :], end[:, :], before[:, 1, :], ALU.subtract)
            then(dve.tensor_tensor(prior[:, :], seen[:, :, CT - 1], here[:, :], ALU.subtract))
            dve.tensor_tensor(gap[:, :], pad_start[:, :], start[:, :], ALU.subtract)
            then(dve.tensor_tensor(offset[:, :], before[:, 0, :], pad_start[:, :], ALU.add))
            then(dve.scalar_tensor_tensor(out=first[:, :], in0=offset[:, :], scalar=-1.0,
                                          in1=prior[:, :], op0=ALU.add, op1=ALU.subtract))

            def by_token(a):
                return a[:, :].unsqueeze(2).to_broadcast([P, EXPERTS, CT])

            then(dve.tensor_tensor(pos[0][:, :, :], seen[:, :, :], by_token(first), ALU.add))
            dve.tensor_tensor(pos[1][:, :, :], pos[0][:, :, :], of[:, :, :], ALU.mult)
            then(dve.tensor_tensor(pos[2][:, :, :], of[:, :, :], by_token(gap), ALU.mult))
            dve.tensor_reduce(slot[:, :], pos[1][:, :, :].rearrange("p e c -> p c e"), AX, ALU.add)
            then(dve.tensor_reduce(shift[:, :], pos[2][:, :, :].rearrange("p e c -> p c e"), AX, ALU.add))
            dve.tensor_copy(place_i[:, 0, :], slot[:, :])
            then(dve.tensor_tensor(rank[:, :], slot[:, :], shift[:, :], ALU.subtract))
            then(dve.tensor_copy(place_i[:, 1, :], rank[:, :]))
            dve.tensor_scalar(low_i[:, :, :], place_i[:, :, :], P - 1, None, ALU.bitwise_and)
            then(dve.tensor_scalar(high_i[:, :, :], place_i[:, :, :], 7, None, ALU.logical_shift_right))
            dve.tensor_copy(low[:, :, :], low_i[:, :, :])
            then(dve.tensor_copy(high[:, :, :], high_i[:, :, :]))

            dve.wait_ge(S["consts"], 9)

            def per(a, n):
                return a.unsqueeze(2).to_broadcast([P, CT, n])

            def across(n):
                return iota_p[:, 0:n].unsqueeze(1).to_broadcast([P, CT, n])

            dve.tensor_tensor(is_low[0][:, :, :], per(low[:, 0, :], P), across(P), ALU.is_equal)
            then(dve.tensor_tensor(is_high[:, :, 0, :], per(high[:, 0, :], STEPS), across(STEPS),
                                   ALU.is_equal))
            dve.tensor_tensor(is_high[:, :, 1, :], is_high[:, :, 0, :], per(token[:, :], STEPS), ALU.mult)
            dve.tensor_tensor(is_high[:, :, 2, :], is_high[:, :, 0, :], per(rank[:, :], STEPS), ALU.mult)\
               .then_inc(S["route_sb"], 1)
            dve.tensor_tensor(is_low[1][:, :, :], per(low[:, 1, :], P), across(P), ALU.is_equal)
            then(dve.tensor_tensor(is_high2[:, :, :], per(high[:, 1, :], TILES), across(TILES),
                                   ALU.is_equal))
            dve.tensor_tensor(is_high2[:, :, :], is_high2[:, :, :], per(token[:, :], TILES), ALU.mult)\
               .then_inc(S["route_sb"], 1)
            dve.tensor_scalar(owner[:, 0, :], tile_at[:, :], pad_end[0:1, 0:1], None, ALU.is_ge)
            then(dve.tensor_scalar(owner[:, 1, :], tile_at[:, :], pad_end[0:1, 1:2], None, ALU.is_ge))
            then(dve.tensor_tensor(owner[:, 0, :], owner[:, 0, :], owner[:, 1, :], ALU.add))
            then(dve.scalar_tensor_tensor(out=owner[:, 2, :], in0=tile_at[:, :],
                                          scalar=pad_end[0:1, 2:3], in1=owner[:, 0, :],
                                          op0=ALU.is_ge, op1=ALU.add))
            dve.tensor_copy(eidx[:, :], owner[:, 2, :])
            dve.wait_ge(S["route_pe"], 2)
            then(dve.tensor_copy(table[:, :, :].rearrange("p a k -> p (a k)"), bank[3][:, 0:3 * STEPS]))
            dve.tensor_copy(gidx[:, :], table[:, 1, :])
            then(dve.tensor_scalar(empty[:, 0, :], table[:, 0, :], -1.0, 1.0, ALU.mult, ALU.add))
            then(dve.tensor_tensor(empty[:, 1, :], empty[:, 0, :], dump[:, :], ALU.mult))
            dve.tensor_tensor(sidx[:, :], empty[:, 1, :], table[:, 2, :], ALU.add)
            dve.wait_ge(S["route_pe"], 3)
            dve.tensor_copy(oidx[:, :], bank[4][:, 0:TILES]).then_inc(S["tables_ready"], 1)

            for n in range(EXPERTS * KC):
                dve.wait_ge(S["ctx_hi"], n + 1)
                dve.tensor_tensor(ctx_w(n // KC, n % KC, 1), ctx_in[:, n // KC, n % KC, :],
                                  ctx_w(n // KC, n % KC, 0).bitcast(F32), ALU.subtract)\
                   .then_inc(S["ctx_lo"], 1)
            dve.wait_ge(S["gates_ready"], 1)
            dve.tensor_scalar(dsb[:, :], dsb[:, :], tg[:, 1:2], None, ALU.mult).then_inc(S["dsb_ready"], 1)

            def stats(m, at):
                dve.bn_stats(bn[:, :], rows[:, ds(at, 1), :]).then_inc(S["bn_parts"], 1)
                dve.wait_ge(S["bn_parts"], m + 1)
                hold(dve)
                dve.bn_aggr(mv[:, :], bn[:, :]).then_inc(S["bn_mv"], 1)
                dve.wait_ge(S["bn_mv"], m + 1)
                dve.tensor_scalar(ve[:, :], mv[:, 1:2], EPS, None, ALU.add)\
                   .then_inc(S["var_ready"], 1)

            def norm(m, at):
                dve.wait_ge(S["rstd_ready"], m + 1)
                dve.wait_ge(S["xt_done"], m) if not isinstance(m, int) or m else None
                dve.tensor_scalar(xn[:, :], rows[:, ds(at, 1), :], mv[:, 0:1], rstd[:, :],
                                  ALU.subtract, ALU.mult).then_inc(S["xn_ready"], 1)

            def x_lo(m, b, u):
                dve.wait_ge(S["xhi_ready"], m + 1)
                dve.tensor_tensor(xpart(b, u, 1), xt_ps[:, :], xpart(b, u, 0).bitcast(F32), ALU.subtract)\
                   .then_inc(S["xlo_ready"], 1)

            def landed(k):
                dve.wait_ge(S["x_landed"], 16 * (k + 1))

            def hidden(k):
                dve.wait_ge(S["silu_ready"], k + 1)
                dve.tensor_tensor(sh[:, :], z_ps[:, :], sh[:, :], ALU.mult).then_inc(S["h_ready"], 1)

            def h_lo(k):
                dve.wait_ge(S["hhi_ready"], k + 1)
                dve.tensor_tensor(hpart(1), ht_ps[:, :], hpart(0).bitcast(F32), ALU.subtract)\
                   .then_inc(S["hlo_ready"], 1)

            def update(k):
                at = ring_slot(k)
                dve.wait_ge(S["y_done"], k + 1)
                dve.scalar_tensor_tensor(out=rows[:, ds(at, 1), :], in0=y_ps[:, :].unsqueeze(1),
                                         scalar=tg[:, 0:1], in1=rows[:, ds(at, 1), :],
                                         op0=ALU.mult, op1=ALU.add).then_inc(S["rows_ready"], 1)

            def piece_lo(q):
                dve.wait_ge(S["piece_hi"], q + 1)
                at = ds(q % 2 * PIECE, PIECE)
                dve.tensor_tensor(wgu[:, ds(q // 2, 1), 1, at], raw[:, ds(q % RAWS, 1), :],
                                  wgu[:, ds(q // 2, 1), 0, at].bitcast(F32), ALU.subtract)\
                   .then_inc(S["piece_lo"], 1)

            landed(0)
            stats(0, ring_slot(0))
            norm(0, ring_slot(0))
            landed(1)
            stats(1, ring_slot(1))
            x_lo(0, 0, 0)
            norm(1, ring_slot(1))
            landed(2)
            stats(2, ring_slot(2))
            hidden(0)
            x_lo(1, 0, 0)
            with dve.Fori(1, PIECES + 1) as k:
                h_lo(k - 1)
                norm(k + 1, ring_slot(k + 1))
                landed(k + 2)
                stats(k + 2, ring_slot(k + 2))
                piece_lo(k - 1)
                hidden(k)
                x_lo(k + 1, 0, 0)
                update(k - 1)
            h_lo(16)
            norm(18, ring_slot(18))
            dve.wait_ge(S["rows_a"], 16)
            stats(19, row_slot(0, 0))
            hidden(17)
            x_lo(18, 0, 0)
            update(16)
            h_lo(17)
            norm(19, row_slot(0, 0))
            stats(20, row_slot(0, 1))
            x_lo(19, 0, 2)
            hidden(18)
            update(17)
            norm(20, row_slot(0, 1))
            dve.wait_ge(S["rows_b"], 16)
            stats(21, row_slot(0, 2))
            h_lo(18)
            x_lo(20, 0, 3)
            norm(21, row_slot(0, 2))
            stats(22, row_slot(0, 3))
            x_lo(21, 0, 0)
            norm(22, row_slot(0, 3))
            update(18)
            x_lo(22, 0, 1)

            def down_lo(c):
                dve.wait_ge(S["down_hi"], c + 1)
                dve.tensor_tensor(down_w(c, 1), rows[:, 2 + c % 4, :], down_w(c, 0).bitcast(F32),
                                  ALU.subtract).then_inc(S["down_lo"], 1)

            def chunk(b, c):
                n = STEPS + IC * b + c
                dve.wait_ge(S["silu_ready"], n + 1)
                dve.wait_ge(S["u_done"], n - STEPS + 1)
                dve.scalar_tensor_tensor(out=sh[:, :], in0=u_ps[:, :], scalar=gs[:, 1, c:c + 1],
                                         in1=sh[:, :], op0=ALU.mult, op1=ALU.mult)\
                   .then_inc(S["h_ready"], 1)
                dve.wait_ge(S["hhi_ready"], n + 1)
                dve.tensor_tensor(hp[:, n_slot(b, c), 1, :], sh[:, :],
                                  hp[:, n_slot(b, c), 0, :].bitcast(F32), ALU.subtract)\
                   .then_inc(S["hlo_ready"], 1)

            def prepare(b, t):
                m = STEPS + BLOCK * b + t
                if t == 0:
                    dve.wait_ge(S["rows_a"], 16 * (b + 1))
                if t == 2:
                    dve.wait_ge(S["rows_b"], 16 * (b + 1))
                stats(m, row_slot(b, t))
                norm(m, row_slot(b, t))
                x_lo(m, b, (t + 2) % BLOCK)

            def finish(b, t):
                n = BLOCK * b + t
                if t == 0:
                    dve.wait_ge(S["d_done"], IC * (b + 1))
                dve.wait_ge(S["rows_ready"], STEPS + n)
                dve.tensor_tensor(tmp[:, :], acc_ps[(t + 2) % BLOCK][:, :], dsb[:, :], ALU.mult)\
                   .then_inc(S["scaled"], 1)
                dve.wait_ge(S["scaled"], n + 1)
                at = row_slot(b, t)
                dve.tensor_tensor(rows[:, at, :], rows[:, at, :], tmp[:, :], ALU.add)\
                   .then_inc(S["rows_ready"], 1)

            for b in range(BLOCKS):
                for c in range(IC):
                    if b == 0:
                        for d in range(3 * c, min(3 * c + 3, IC)):
                            down_lo(d)
                    chunk(b, c)
                    if c in PREP_AT and b + 1 < BLOCKS:
                        prepare(b + 1, PREP_AT[c])
                for t in range(BLOCK):
                    finish(b, t)

        @block.tensor
        def _(pe):
            pe.wait_ge(S["consts"], 9)
            pe.wait_ge(S["route_sb"], 1)
            pe.matmul(bank[2][:, 0:EXPERTS], tri[:, :], here16[:, :], start=True, stop=True)
            pe.matmul(bank[2][:, EXPERTS:2 * EXPERTS], ones16[:, :], here16[:, :], start=True, stop=True)\
              .then_inc(S["route_pe"], 1)
            pe.wait_ge(S["route_sb"], 2)
            for c in range(CT):
                mm = pe.matmul(bank[3][:, 0:3 * STEPS], is_low[0][:, c, :],
                               is_high[:, c, :, :].rearrange("p a k -> p (a k)"),
                               start=c == 0, stop=c == CT - 1)
            mm.then_inc(S["route_pe"], 1)
            pe.wait_ge(S["route_sb"], 3)
            for c in range(CT):
                mm = pe.matmul(bank[4][:, 0:TILES], is_low[1][:, c, :], is_high2[:, c, :],
                               start=c == 0, stop=c == CT - 1)
            mm.then_inc(S["route_pe"], 1)

            def turn_x(m):
                pe.wait_ge(S["xn_ready"], m + 1)
                if not isinstance(m, int) or m:
                    pe.wait_ge(S["xlo_ready"], m)
                for c in range(KC):
                    mm = pe.transpose(xt_ps[:, c * P:(c + 1) * P], xn[:, c * P:(c + 1) * P], ident[:, :])
                mm.then_inc(S["xt_done"], 1)

            def expert_product(out_ps, part, e):
                last = len(PASSES) * KC - 1
                for n in range(last + 1):
                    (s, w), c = PASSES[n // KC], n % KC
                    mm = pe.matmul(out_ps[:, :], part(s)[:, c * P:(c + 1) * P], ctx_w(e, c, w),
                                   start=n == 0, stop=n == last)
                return mm

            def expert(k):
                return pe.value_load(eidx[0:1, ds(k, 1)], min_val=0, max_val=EXPERTS - 1)

            def first_product(k):
                pe.wait_ge(S["xlo_ready"], k + 1)
                expert_product(z_ps, lambda s: xpart(0, 0, s), expert(k)).then_inc(S["z_done"], 1)

            def turn_h(k):
                pe.wait_ge(S["h_ready"], k + 1)
                for c in range(KC):
                    mm = pe.transpose(ht_ps[:, c * P:(c + 1) * P], sh[:, c * P:(c + 1) * P], ident[:, :])
                mm.then_inc(S["ht_done"], 1)

            def second_product(k):
                pe.wait_ge(S["hlo_ready"], k + 1)
                if not isinstance(k, int) or k:
                    pe.wait_ge(S["rows_ready"], k)
                expert_product(y_ps, hpart, expert(k)).then_inc(S["y_done"], 1)

            turn_x(0)
            pe.wait_ge(S["tables_ready"], 1)
            pe.wait_ge(S["ctx_lo"], EXPERTS * KC)
            first_product(0)
            turn_x(1)
            turn_h(0)
            with pe.Fori(1, PIECES + 1) as k:
                first_product(k)
                turn_x(k + 1)
                second_product(k - 1)
                turn_h(k)
            first_product(17)
            turn_x(18)
            second_product(16)
            turn_h(17)
            first_product(18)
            turn_x(19)
            second_product(17)
            turn_h(18)
            turn_x(20)
            turn_x(21)
            second_product(18)
            turn_x(22)

            def inner_product(out_ps, b, row, c):
                last = len(PASSES) * KC - 1
                for n in range(last + 1):
                    (w, s), h = PASSES[n // KC], n % KC
                    moving = xbuf(b).rearrange("p (u s h j) -> p s h u j", u=BLOCK, s=2, h=KC)[:, s, h]
                    mm = pe.matmul(out_ps[:, :], wgu[:, row + h, w, c * P:(c + 1) * P], moving,
                                   start=n == 0, stop=n == last)
                return mm

            def down_product(b, c):
                n = IC * b + c
                pe.wait_ge(S["hlo_ready"], STEPS + n + 1)
                pe.wait_ge(S["down_lo"], c + 1)
                if c == 0:
                    pe.wait_ge(S["rows_ready"], STEPS + BLOCK * b)
                for u in range(BLOCK):
                    for n_, (s, w) in enumerate(PASSES):
                        mm = pe.matmul(acc_ps[u][:, :], hp[:, n_slot(b, c), s, u * P:(u + 1) * P],
                                       down_w(c, w), start=c == 0 and n_ == 0,
                                       stop=c == IC - 1 and n_ == len(PASSES) - 1)
                mm.then_inc(S["d_done"], 1)

            for b in range(BLOCKS):
                pe.wait_ge(S["xlo_ready"], STEPS + BLOCK * (b + 1))
                for c in range(IC):
                    n = STEPS + IC * b + c
                    pe.wait_ge(S["silu_ready"], n)
                    if c == 0:
                        pe.wait_ge(S["h_ready"], n)
                    inner_product(g_ps, b, 0, c).then_inc(S["z_done"], 1)
                    pe.wait_ge(S["h_ready"], n)
                    if n == STEPS:
                        pe.wait_ge(S["rows_ready"], STEPS)
                    inner_product(u_ps, b, KC, c).then_inc(S["u_done"], 1)
                    if c in PREP_AT and b + 1 < BLOCKS:
                        turn_x(STEPS + BLOCK * (b + 1) + PREP_AT[c])
                    if c:
                        down_product(b, c - 1)
                down_product(b, IC - 1)


def n_slot(b, c):
    return (IC * b + c) % 2


def kernel(x, itok_BxS_13_99985, ctx_2048, g_xattn, g_ffn, L0_ffn_gate_w, L0_ffn_up_w,
           L0_ffn_down_w, L0_ffn_gate_s, L0_ffn_up_s, L0_ffn_down_s):
    import numpy as np
    import concourse.bacc as bacc
    from concourse.bass_utils import run_bass_kernel_spmd

    x, ids, ctx, gate, up, down = (np.asarray(a) for a in (
        x, itok_BxS_13_99985, ctx_2048, L0_ffn_gate_w, L0_ffn_up_w, L0_ffn_down_w))
    arrays = {
        "x": np.ascontiguousarray(x.reshape(TOKENS, D)),
        "ids": np.ascontiguousarray(ids.reshape(P, CT)),
        "ctxT": np.ascontiguousarray(ctx.transpose(0, 2, 1)),
        "g_x": np.asarray(g_xattn),
        "g_f": np.asarray(g_ffn),
        "guT": np.ascontiguousarray(np.concatenate([gate.T, up.T])),
        "dwT": np.ascontiguousarray(down.T),
        "gate_s": np.ascontiguousarray(np.asarray(L0_ffn_gate_s).reshape(IC, P).T),
        "up_s": np.ascontiguousarray(np.asarray(L0_ffn_up_s).reshape(IC, P).T),
        "down_s": np.asarray(L0_ffn_down_s),
    }
    nc = bacc.Bacc("TRN2", target_bir_lowering=False, num_devices=1)
    args = [nc.dram_tensor(n, a.shape, mybir.dt.from_np(a.dtype), kind="ExternalInput").ap()
            for n, a in arrays.items()]
    out = nc.dram_tensor("out", (TOKENS, D), F32, kind="ExternalOutput").ap()
    build(nc, *args, out)
    r = run_bass_kernel_spmd(nc, [arrays], core_ids=[0])
    return r.results[0]["out"].reshape(4, TOKENS // 4, D)
```

```python
from contextlib import ExitStack

import concourse.bass as bass
from concourse import mybir
from concourse.bass import ds

F32 = mybir.dt.float32
F32R = mybir.dt.float32r
FP16 = mybir.dt.float16
I32 = mybir.dt.int32
U32 = mybir.dt.uint32
ALU = mybir.AluOpType
ACT = mybir.ActivationFunctionType
AX = mybir.AxisListType.X

P = 128
TOKENS = 2048
D = 512
KC = D // P
EXPERTS = 4
VOCAB = 25000
PER_EXPERT = VOCAB // EXPERTS
TILES = TOKENS // P
STEPS = TILES + EXPERTS - 1
CT = TOKENS // P
INTER = 1408
IC = INTER // P
BLOCK = 4
BLOCKS = TILES // BLOCK
PIECE = INTER // 2
PIECES = 2 * KC * 2
RING = 6
ROWS = 8
RAWS = 4
EPS = 1e-5
LO_BITS = (1 << 12) - 1
PASSES = [(0, 0), (1, 0), (0, 1)]
CTX_WORDS = EXPERTS * KC * 2 * D
XBUF_WORDS = BLOCK * 2 * D
PREP_AT = {5: 0, 6: 1, 7: 2, 8: 3}


def ring_slot(k):
    return (k + 4) % RING


def row_slot(b, t):
    return (RING + BLOCK * b + t) % ROWS


def build(nc, x, ids, ctxT, g_x, g_f, guT, dwT, gate_s, up_s, down_s, out):
    scratch = nc.dram_tensor("x1_rows", [2 * TOKENS + STEPS * P, D], F32).ap()
    ctx_v = ctxT.rearrange("e (c p) f -> e p c f", p=P)
    gu_v = guT.rearrange("(r p) (v n) -> p r v n", p=P, v=2)
    dw_v = dwT.rearrange("(c p) h -> c p h", p=P)
    x1_v = scratch[0:TOKENS, :].rearrange("(t p) h -> p t h", p=P)

    with ExitStack() as ctx:
        def sb(name, shape, dt):
            return ctx.enter_context(nc.sbuf_tensor(name, shape, dt))

        def psum(name):
            return ctx.enter_context(nc.psum_tensor(name, [P, D], F32))

        def sem(name):
            return ctx.enter_context(nc.semaphore(name))

        work_base = (nc.sbuf_base + 31) // 32 * 32
        work = sb("work", [P, CTX_WORDS + XBUF_WORDS], F32R)
        wgu_base = nc.sbuf_base
        wgu = sb("wgu", [P, 2 * KC, 2, INTER], F32R)
        raw_base = nc.sbuf_base
        raw = sb("raw", [P, RAWS, PIECE], F32)
        rows = sb("rows", [P, ROWS, D], F32)
        xn = sb("xn", [P, D], F32)
        sh = sb("sh", [P, D], F32)
        tmp = sb("tmp", [P, D], F32)
        dsb = sb("dsb", [P, D], F32)
        ident = sb("ident", [P, P], F32)
        bn = sb("bn", [P, 6], F32)
        mv = sb("mv", [P, 2], F32)
        ve = sb("ve", [P, 1], F32)
        rstd = sb("rstd", [P, 1], F32)
        half = sb("half", [P, 1], F32)
        gs = sb("gs", [P, 2, IC], F32)
        lo_sums = sb("lo_sums", [P, PIECES], F32)
        loose = sb("loose", [P, 4], F32)
        flag = sb("flag", [1, 1], I32)
        gg = sb("gg", [P, 2], F32)
        tg = sb("tg", [P, 2], F32)
        gidx = sb("gidx", [P, STEPS], U32)
        sidx = sb("sidx", [P, STEPS], U32)
        oidx = sb("oidx", [P, TILES], U32)
        eidx = sb("eidx", [1, STEPS], I32)
        inow = sb("inow", [P, 2], U32)


        hp = [nc.alloc_sbuf_tensor_at(f"hp{n}", [P, 2, D], F32R, offset=at) for n, at in enumerate(
            (raw_base, raw_base + 2 * D * 4, work_base + IC * 2 * D * 4))]
        spare = work_base + (CTX_WORDS + XBUF_WORDS // 2) * 4
        checked = nc.alloc_sbuf_tensor_at("checked", [P, 2, D], I32, offset=spare)
        junk = nc.alloc_sbuf_tensor_at("junk", [P, PIECE], F32, offset=spare + 2 * D * 4)
        low_bits = tmp[:, :].bitcast(I32)
        wgu_bytes = 2 * KC * 2 * INTER * 4
        ctx_in_bytes = EXPERTS * KC * D * 4
        ctx_in = nc.alloc_sbuf_tensor_at("ctx_in", [P, EXPERTS, KC, D], F32,
                                         offset=wgu_base + wgu_bytes - ctx_in_bytes)
        route_at = [wgu_base + 3 * 2 * INTER * 4]

        def rt(name, shape, dt):
            count = 1
            for n in shape[1:]:
                count *= n
            at = route_at[0]
            route_at[0] = (at + count * (2 if dt == FP16 else 4) + 31) // 32 * 32
            assert route_at[0] <= wgu_base + wgu_bytes - ctx_in_bytes
            return nc.alloc_sbuf_tensor_at(name, shape, dt, offset=at)

        ids_i = rt("ids_i", [P, CT], I32)
        ids_f = rt("ids_f", [P, CT], F32)
        at_least = rt("at_least", [P, EXPERTS + 1, CT], F32)
        of = rt("of", [P, EXPERTS, CT], F32)
        ones_f = rt("ones_f", [P, EXPERTS * CT], F32)
        seen = rt("seen", [P, EXPERTS, CT], F32)
        here = rt("here", [P, EXPERTS], F32)
        here16 = rt("here16", [P, EXPERTS], FP16)
        tri = rt("tri", [P, P], FP16)
        ones16 = rt("ones16", [P, P], FP16)
        before = rt("before", [P, 2, EXPERTS], F32)
        pad_i = rt("pad_i", [P, EXPERTS], I32)
        pad = rt("pad", [P, EXPERTS], F32)
        pad_end = rt("pad_end", [P, EXPERTS], F32)
        end = rt("end", [P, EXPERTS], F32)
        small = [rt(f"small{n}", [P, EXPERTS], F32) for n in range(6)]
        pos = [rt(f"pos{n}", [P, EXPERTS, CT], F32) for n in range(3)]
        slot = rt("slot", [P, CT], F32)
        shift = rt("shift", [P, CT], F32)
        rank = rt("rank", [P, CT], F32)
        place_i = rt("place_i", [P, 2, CT], I32)
        low_i = rt("low_i", [P, 2, CT], I32)
        high_i = rt("high_i", [P, 2, CT], I32)
        low = rt("low", [P, 2, CT], F32)
        high = rt("high", [P, 2, CT], F32)
        iota_p = rt("iota_p", [P, P], F32)
        token = rt("token", [P, CT], F32)
        dump = rt("dump", [P, STEPS], F32)
        tile_at = rt("tile_at", [1, STEPS], F32)
        is_low = [rt(f"is_low{n}", [P, CT, P], FP16) for n in range(2)]
        is_high = rt("is_high", [P, CT, 3, STEPS], FP16)
        is_high2 = rt("is_high2", [P, CT, TILES], FP16)
        table = rt("table", [P, 3, STEPS], F32)
        empty = rt("empty", [P, 2, STEPS], F32)
        owner = rt("owner", [1, 3, STEPS], F32)

        bank = [psum(f"bank{n}") for n in range(8)]
        z_ps, y_ps, g_ps, u_ps = bank[0], bank[1], bank[0], bank[1]
        acc_ps = bank[2:6]
        xt_ps, ht_ps = bank[6], bank[7]

        def hslot(c):
            return hp[2 if c == IC - 1 else c % 2]

        def xbuf(b):
            base = CTX_WORDS - XBUF_WORDS * (b % 2)
            return work[:, ds(base, XBUF_WORDS)]

        def xpart(b, u, s):
            base = CTX_WORDS - XBUF_WORDS * (b % 2)
            return work[:, ds(base + (2 * u + s) * D, D)]

        def hpart(s):
            return work[:, CTX_WORDS + (2 + s) * D:CTX_WORDS + (3 + s) * D]

        def ctx_w(e, c, s):
            return work[:, ds(e * (KC * 2 * D) + (c * 2 + s) * D, D)]

        def down_w(c, s):
            return work[:, (c * 2 + s) * D:(c * 2 + s + 1) * D]

        names = """ids_in small_in consts route_pe route_sb route_step tables_ready
            piece_landed piece_hi piece_lo down_hi down_lo x_landed stored rows_a rows_b
            bn_parts bn_mv var_ready rstd_ready xn_ready xt_done xhi_ready xlo_ready
            z_done y_done silu_ready h_ready ht_done hhi_ready hlo_ready u_done d_done rows_ready
            scaled gates_ready dsb_ready ctx_hi ctx_lo out_stored index_now held
            check_landed bits_done sums_done loose_step loose_ready loose_counted flag_ready
            acc_done oidx_ready table_loaded""".split()
        S = {n: sem(n) for n in names}
        ctx_landed = [sem(f"ctx_landed{e}") for e in range(EXPERTS)]
        down_landed = [sem(f"down_landed{n}") for n in range(4)]
        last_stored = [sem(f"last_stored{t}") for t in range(BLOCK)]

        def hold(eng):
            eng.sem_inc(S["held"])

        block = ctx.enter_context(nc.Block())

        @block.sync
        def _(sp):
            sp.dma_start(ids_i[:, :], ids).then_inc(S["ids_in"], 16)
            for e in range(EXPERTS):
                sp.dma_start(ctx_in[:, e], ctx_v[e]).then_inc(ctx_landed[e], 16)
            for s, src in enumerate((gate_s, up_s)):
                sp.dma_start(gs[:, s, :], src).then_inc(S["small_in"], 16)
            sp.wait_ge(S["table_loaded"], 1)
            for s, src in enumerate((g_x, g_f)):
                sp.dma_start(gg[:, s:s + 1], src.partition_broadcast(P)).then_inc(S["small_in"], 16)
            sp.dma_start(dsb[:, :], down_s.partition_broadcast(P)).then_inc(S["small_in"], 16)

            def piece_at(q):
                return sp.snap(q % RAWS), sp.snap(q // 2), sp.snap(q % 2), sp.snap(q - RAWS + 1), sp.snap(16 * q)

            def piece(at, row, half_):
                sp.dma_start(raw[:, ds(at, 1), :], gu_v[:, ds(row, 1), ds(half_, 1), :])\
                  .then_inc(S["piece_landed"], 16)

            for q in range(RAWS):
                if q:
                    sp.wait_ge(S["piece_landed"], 16 * q)
                piece(q % RAWS, q // 2, q % 2)

            def check_row(c):
                sp.dma_start(checked[:, ds(c % 2, 1), :], dw_v[ds(c, 1)].bitcast(I32)
                             .rearrange("c p h -> p c h")).then_inc(S["check_landed"], 16)

            check_row(0)
            sp.wait_ge(S["check_landed"], 16)
            check_row(1)

            def next_piece(q):
                *at, split, all_before = piece_at(q)
                sp.wait_ge(S["piece_landed"], all_before)
                hold(sp)
                sp.wait_ge(S["piece_lo"], split)
                hold(sp)
                piece(*at)

            with sp.Fori(RAWS, RAWS + IC - 2) as q:
                next_piece(q)
                c, c_before, c_checked = sp.snap(q - 2), sp.snap(16 * (q - 2)), sp.snap(q - 2)
                sp.wait_ge(S["check_landed"], c_before)
                hold(sp)
                sp.wait_ge(S["bits_done"], c_checked)
                hold(sp)
                check_row(c)
            with sp.Fori(RAWS + IC - 2, PIECES) as q:
                next_piece(q)

            def load_rows(b):
                for half_, landed in enumerate((S["rows_a"], S["rows_b"])):
                    t = BLOCK * b + 2 * half_
                    at = row_slot(b, 2 * half_)
                    sp.dma_start(rows[:, at:at + 2, :], x1_v[:, t:t + 2, :]).then_inc(landed, 16)
                    if b == 0 and half_ == 0:
                        sp.wait_ge(S["stored"], 16 * 16)

            sp.wait_ge(S["stored"], 16 * (BLOCK + EXPERTS - 1))
            load_rows(0)
            sp.wait_ge(S["stored"], 16 * STEPS)
            for c in range(IC):
                if c >= 4:
                    sp.wait_ge(S["down_lo"], c - 3)
                sp.dma_start(rows[:, 2 + c % 4, :], dw_v[c]).then_inc(down_landed[c % 4], 16)
            sp.wait_ge(S["down_lo"], IC)
            load_rows(1)
            for b in range(2, BLOCKS):
                sp.wait_ge(S["out_stored"], 16 * BLOCK * (b - 1))
                load_rows(b)
            sp.wait_ge(S["out_stored"], 16 * BLOCK * (BLOCKS - 1))
            for t in range(BLOCK):
                sp.wait_ge(last_stored[t], 16)

        @block.gpsimd
        def _(pool):
            pool.memset(half[:, :], -0.5).then_inc(S["consts"], 1)
            pool.memset(ident[:, :], 0.0).then_inc(S["consts"], 1)
            pool.memset(ones16[:, :], 1.0).then_inc(S["consts"], 1)
            pool.wait_ge(S["consts"], 3)
            pool.affine_select(out=ident[:, :], in_=ident[:, :], compare_op=ALU.not_equal, fill=1.0,
                               base=0, pattern=[[-1, P]], channel_multiplier=1).then_inc(S["consts"], 1)
            pool.affine_select(out=tri[:, :], in_=ones16[:, :], compare_op=ALU.is_gt, fill=0.0,
                               base=0, pattern=[[1, P]], channel_multiplier=-1).then_inc(S["consts"], 1)
            exact = dict(allow_small_or_imprecise_dtypes=True)
            pool.iota(iota_p[:, :], pattern=[[1, P]], base=0, channel_multiplier=0, **exact)\
                .then_inc(S["consts"], 1)
            pool.iota(token[:, :], pattern=[[1, CT]], base=0, channel_multiplier=CT, **exact)\
                .then_inc(S["consts"], 1)
            pool.iota(dump[:, :], pattern=[[P, STEPS]], base=TOKENS, channel_multiplier=1, **exact)\
                .then_inc(S["consts"], 1)
            pool.iota(tile_at[:, :], pattern=[[P, STEPS]], base=0, channel_multiplier=0, **exact)\
                .then_inc(S["consts"], 1)
            pool.wait_ge(S["consts"], 9)

            def gather(at, index):
                pool.indirect_dma_start(
                    rows[:, at, :], None, x, bass.IndirectOffsetOnAxis(ap=index, axis=0))\
                    .then_inc(S["x_landed"], 16)

            def store(at, index):
                pool.indirect_dma_start(
                    scratch, bass.IndirectOffsetOnAxis(ap=index, axis=0), rows[:, at, :], None)\
                    .then_inc(S["stored"], 16)

            def inverse_std(m):
                pool.wait_ge(S["var_ready"], m + 1)
                pool.tensor_tensor(rstd[:, :], ve[:, :], half[:, :], ALU.pow)\
                    .then_inc(S["rstd_ready"], 1)

            pool.wait_ge(S["tables_ready"], 1)
            for k in range(5):
                if k:
                    pool.wait_ge(S["x_landed"], 16 * k)
                gather(ring_slot(k), gidx[:, k:k + 1])
                if k >= 1:
                    inverse_std(k - 1) if k <= 2 else None
            inverse_std(2)
            inverse_std(3)
            pool.wait_ge(S["x_landed"], 16 * 5)
            gather(ring_slot(5), gidx[:, 5:6])
            pool.wait_ge(S["rows_ready"], 1)
            store(ring_slot(0), sidx[:, 0:1])

            with pool.Fori(0, 2) as i:
                for j in range(RING):
                    k = 2 + RING * i + j
                    inverse_std(k + 2)
                    pool.wait_ge(S["x_landed"], 16 * (k + 4))
                    pool.tensor_copy(inow[:, 0:1], gidx[:, ds(k + 4, 1)]).then_inc(S["index_now"], 1)
                    pool.wait_ge(S["stored"], 16 * (k - 1))
                    pool.tensor_copy(inow[:, 1:2], sidx[:, ds(k - 1, 1)]).then_inc(S["index_now"], 1)
                    pool.wait_ge(S["index_now"], 2 * (k - 1))
                    hold(pool)
                    gather(ring_slot(2 + j + 4), inow[:, 0:1])
                    pool.wait_ge(S["rows_ready"], k)
                    hold(pool)
                    store(ring_slot(2 + j - 1), inow[:, 1:2])
            for k in range(14, STEPS + 1):
                inverse_std(k + 2)
                if k == STEPS:
                    inverse_std(k + 3)
                if k + 4 < STEPS:
                    pool.wait_ge(S["stored"], 16 * (k - 1))
                    pool.wait_ge(S["x_landed"], 16 * (k + 4))
                    gather(ring_slot(k + 4), gidx[:, k + 4:k + 5])
                pool.wait_ge(S["stored"], 16 * (k - 1))
                pool.wait_ge(S["rows_ready"], k)
                store(ring_slot(k - 1), sidx[:, k - 1:k])

            pool.wait_ge(S["oidx_ready"], 1)
            for b in range(BLOCKS):
                if b + 1 < BLOCKS:
                    for t in range(BLOCK):
                        inverse_std(STEPS + BLOCK * (b + 1) + t)
                for u in range(BLOCK):
                    n, t = BLOCK * b + u, (u + 2) % BLOCK
                    pool.wait_ge(S["rows_ready"], STEPS + n + 1)
                    if b + 1 < BLOCKS:
                        if n:
                            pool.wait_ge(S["out_stored"], 16 * n)
                        done = S["out_stored"]
                    else:
                        done = last_stored[t]
                    pool.indirect_dma_start(
                        out, bass.IndirectOffsetOnAxis(ap=oidx[:, BLOCK * b + t:BLOCK * b + t + 1], axis=0),
                        rows[:, row_slot(b, t), :], None).then_inc(done, 16)

        @block.scalar
        def _(act):
            act.wait_ge(S["consts"], 1)
            act.activation(gg[:, 0:1], half[:, :], ACT.Silu).then_inc(S["table_loaded"], 1)
            for e in range(EXPERTS):
                act.wait_ge(ctx_landed[e], 16)
                for c in range(KC):
                    act.activation(ctx_w(e, c, 0), ctx_in[:, e, c, :], ACT.Copy).then_inc(S["ctx_hi"], 1)
            act.wait_ge(S["small_in"], 16 * 5)
            act.activation(tg[:, :], gg[:, :], ACT.Tanh).then_inc(S["gates_ready"], 1)

            def x_hi(m, b, u):
                act.wait_ge(S["xt_done"], m + 1)
                act.activation(xpart(b, u, 0), xt_ps[:, :], ACT.Copy).then_inc(S["xhi_ready"], 1)

            def h_hi(k):
                act.wait_ge(S["ht_done"], k + 1)
                act.activation(hpart(0), ht_ps[:, :], ACT.Copy).then_inc(S["hhi_ready"], 1)

            def silu(k):
                act.wait_ge(S["z_done"], k + 1)
                act.activation(sh[:, :], z_ps[:, :], ACT.Silu).then_inc(S["silu_ready"], 1)

            def piece_hi(q):
                act.wait_ge(S["piece_landed"], 16 * (q + 1))
                act.activation(wgu[:, ds(q // 2, 1), 0, ds(q % 2 * PIECE, PIECE)],
                               raw[:, ds(q % RAWS, 1), :], ACT.Copy).then_inc(S["piece_hi"], 1)

            def piece_sum(q):
                act.wait_ge(S["piece_lo"], q + 1)
                act.activation(junk[:, :], wgu[:, ds(q // 2, 1), 1, ds(q % 2 * PIECE, PIECE)].bitcast(F32),
                               ACT.Abs, accum_out=lo_sums[:, ds(q, 1)]).then_inc(S["sums_done"], 1)

            x_hi(0, 0, 0)
            silu(0)
            x_hi(1, 0, 0)
            with act.Fori(1, PIECES + 1) as k:
                h_hi(k - 1)
                piece_hi(k - 1)
                silu(k)
                x_hi(k + 1, 0, 0)
                piece_sum(k - 1)
            h_hi(16)
            silu(17)
            x_hi(18, 0, 0)
            h_hi(17)
            x_hi(19, 0, 2)
            silu(18)
            h_hi(18)
            x_hi(20, 0, 3)
            x_hi(21, 0, 0)
            act.wait_ge(S["y_done"], STEPS)
            x_hi(22, 0, 1)

            def down_hi(c):
                act.wait_ge(down_landed[c % 4], 16 * (c // 4 + 1))
                act.activation(down_w(c, 0), rows[:, 2 + c % 4, :], ACT.Copy).then_inc(S["down_hi"], 1)

            def chunk(b, c):
                n = STEPS + IC * b + c
                act.wait_ge(S["z_done"], n + 1)
                act.wait_ge(S["hlo_ready"], n)
                act.activation(sh[:, :], g_ps[:, :], ACT.Silu, scale=gs[:, 0, c:c + 1])\
                   .then_inc(S["silu_ready"], 1)
                act.wait_ge(S["h_ready"], n + 1)
                act.activation(hslot(c)[:, 0, :], sh[:, :], ACT.Copy).then_inc(S["hhi_ready"], 1)

            def mlp_block(b, first=False, last=False):
                for c in range(IC):
                    chunk(b, c)
                    if first:
                        for d in range(3 * c, min(3 * c + 3, IC)):
                            down_hi(d)
                    if c - 1 in PREP_AT and not last:
                        t = PREP_AT[c - 1]
                        x_hi(STEPS + BLOCK * (b + 1) + t, b + 1, (t + 2) % BLOCK)

            mlp_block(0, first=True)
            with act.Fori(1, BLOCKS - 1) as b:
                mlp_block(b)
            mlp_block(BLOCKS - 1, last=True)

        @block.vector
        def _(dve):
            steps = [0]

            def then(ins):
                steps[0] += 1
                ins.then_inc(S["route_step"], 1)
                dve.wait_ge(S["route_step"], steps[0])

            dve.memset(at_least[:, 0, :], 1.0)
            dve.memset(at_least[:, EXPERTS, :], 0.0)
            dve.memset(ones_f[:, :], 1.0)
            dve.wait_ge(S["ids_in"], 16)
            then(dve.tensor_copy(ids_f[:, :], ids_i[:, :]))
            for e in range(1, EXPERTS):
                ins = dve.tensor_scalar(at_least[:, e, :], ids_f[:, :], float(PER_EXPERT * e), None,
                                        ALU.is_ge)
            then(ins)
            then(dve.tensor_tensor(of[:, :, :], at_least[:, 0:EXPERTS, :], at_least[:, 1:EXPERTS + 1, :],
                                   ALU.subtract))
            dve.tensor_tensor_scan(seen[:, :, :].rearrange("p e c -> p (e c)"), ones_f[:, :],
                                   of[:, :, :].rearrange("p e c -> p (e c)"), 0.0, ALU.mult, ALU.add)
            then(dve.tensor_reduce(here[:, :], of[:, :, :], AX, ALU.add))
            dve.tensor_copy(here16[:, :], here[:, :]).then_inc(S["route_sb"], 1)
            dve.wait_ge(S["route_pe"], 1)
            then(dve.tensor_copy(before[:, :, :].rearrange("p a e -> p (a e)"), bank[2][:, 0:2 * EXPERTS]))
            then(dve.tensor_scalar(pad_i[:, :], before[:, 1, :], float(P - 1), None, ALU.add))
            then(dve.tensor_scalar(pad_i[:, :], pad_i[:, :], -P, None, ALU.bitwise_and))
            then(dve.tensor_copy(pad[:, :], pad_i[:, :]))
            dve.tensor_tensor_scan(pad_end[:, :], ones_f[:, 0:EXPERTS], pad[:, :], 0.0, ALU.mult, ALU.add)
            then(dve.tensor_tensor_scan(end[:, :], ones_f[:, 0:EXPERTS], before[:, 1, :], 0.0,
                                        ALU.mult, ALU.add))
            pad_start, start, offset, prior, first, gap = small
            dve.tensor_tensor(pad_start[:, :], pad_end[:, :], pad[:, :], ALU.subtract)
            dve.tensor_tensor(start[:, :], end[:, :], before[:, 1, :], ALU.subtract)
            then(dve.tensor_tensor(prior[:, :], seen[:, :, CT - 1], here[:, :], ALU.subtract))
            dve.tensor_tensor(gap[:, :], pad_start[:, :], start[:, :], ALU.subtract)
            then(dve.tensor_tensor(offset[:, :], before[:, 0, :], pad_start[:, :], ALU.add))
            then(dve.scalar_tensor_tensor(out=first[:, :], in0=offset[:, :], scalar=-1.0,
                                          in1=prior[:, :], op0=ALU.add, op1=ALU.subtract))

            def by_token(a):
                return a[:, :].unsqueeze(2).to_broadcast([P, EXPERTS, CT])

            then(dve.tensor_tensor(pos[0][:, :, :], seen[:, :, :], by_token(first), ALU.add))
            dve.tensor_tensor(pos[1][:, :, :], pos[0][:, :, :], of[:, :, :], ALU.mult)
            then(dve.tensor_tensor(pos[2][:, :, :], of[:, :, :], by_token(gap), ALU.mult))
            dve.tensor_reduce(slot[:, :], pos[1][:, :, :].rearrange("p e c -> p c e"), AX, ALU.add)
            then(dve.tensor_reduce(shift[:, :], pos[2][:, :, :].rearrange("p e c -> p c e"), AX, ALU.add))
            dve.tensor_copy(place_i[:, 0, :], slot[:, :])
            then(dve.tensor_tensor(rank[:, :], slot[:, :], shift[:, :], ALU.subtract))
            then(dve.tensor_copy(place_i[:, 1, :], rank[:, :]))
            dve.tensor_scalar(low_i[:, :, :], place_i[:, :, :], P - 1, None, ALU.bitwise_and)
            then(dve.tensor_scalar(high_i[:, :, :], place_i[:, :, :], 7, None, ALU.logical_shift_right))
            dve.tensor_copy(low[:, :, :], low_i[:, :, :])
            then(dve.tensor_copy(high[:, :, :], high_i[:, :, :]))

            dve.wait_ge(S["consts"], 9)

            def per(a, n):
                return a.unsqueeze(2).to_broadcast([P, CT, n])

            def across(n):
                return iota_p[:, 0:n].unsqueeze(1).to_broadcast([P, CT, n])

            dve.tensor_tensor(is_low[0][:, :, :], per(low[:, 0, :], P), across(P), ALU.is_equal)
            then(dve.tensor_tensor(is_high[:, :, 0, :], per(high[:, 0, :], STEPS), across(STEPS),
                                   ALU.is_equal))
            dve.tensor_tensor(is_high[:, :, 1, :], is_high[:, :, 0, :], per(token[:, :], STEPS), ALU.mult)
            dve.tensor_tensor(is_high[:, :, 2, :], is_high[:, :, 0, :], per(rank[:, :], STEPS), ALU.mult)\
               .then_inc(S["route_sb"], 1)
            dve.tensor_scalar(owner[:, 0, :], tile_at[:, :], pad_end[0:1, 0:1], None, ALU.is_ge)
            then(dve.tensor_scalar(owner[:, 1, :], tile_at[:, :], pad_end[0:1, 1:2], None, ALU.is_ge))
            then(dve.tensor_tensor(owner[:, 0, :], owner[:, 0, :], owner[:, 1, :], ALU.add))
            then(dve.scalar_tensor_tensor(out=owner[:, 2, :], in0=tile_at[:, :],
                                          scalar=pad_end[0:1, 2:3], in1=owner[:, 0, :],
                                          op0=ALU.is_ge, op1=ALU.add))
            dve.tensor_copy(eidx[:, :], owner[:, 2, :])
            dve.wait_ge(S["route_pe"], 2)
            then(dve.tensor_copy(table[:, :, :].rearrange("p a k -> p (a k)"), bank[3][:, 0:3 * STEPS]))
            dve.tensor_copy(gidx[:, :], table[:, 1, :])
            then(dve.tensor_scalar(empty[:, 0, :], table[:, 0, :], -1.0, 1.0, ALU.mult, ALU.add))
            then(dve.tensor_tensor(empty[:, 1, :], empty[:, 0, :], dump[:, :], ALU.mult))
            dve.tensor_tensor(sidx[:, :], empty[:, 1, :], table[:, 2, :], ALU.add)\
               .then_inc(S["tables_ready"], 1)
            dve.memset(low_bits, 0).then_inc(S["bits_done"], 1)

            def ctx_lo(n):
                dve.wait_ge(S["ctx_hi"], n + 1)
                dve.tensor_tensor(ctx_w(n // KC, n % KC, 1), ctx_in[:, n // KC, n % KC, :],
                                  ctx_w(n // KC, n % KC, 0).bitcast(F32), ALU.subtract)\
                   .then_inc(S["ctx_lo"], 1)

            def stats(m, at):
                dve.bn_stats(bn[:, :], rows[:, ds(at, 1), :]).then_inc(S["bn_parts"], 1)
                dve.wait_ge(S["bn_parts"], m + 1)
                hold(dve)
                dve.bn_aggr(mv[:, :], bn[:, :]).then_inc(S["bn_mv"], 1)
                dve.wait_ge(S["bn_mv"], m + 1)
                dve.tensor_scalar(ve[:, :], mv[:, 1:2], EPS, None, ALU.add)\
                   .then_inc(S["var_ready"], 1)

            def norm(m, at):
                dve.wait_ge(S["rstd_ready"], m + 1)
                dve.wait_ge(S["xt_done"], m) if not isinstance(m, int) or m else None
                dve.tensor_scalar(xn[:, :], rows[:, ds(at, 1), :], mv[:, 0:1], rstd[:, :],
                                  ALU.subtract, ALU.mult).then_inc(S["xn_ready"], 1)

            def x_lo(m, b, u):
                dve.wait_ge(S["xhi_ready"], m + 1)
                dve.tensor_tensor(xpart(b, u, 1), xt_ps[:, :], xpart(b, u, 0).bitcast(F32), ALU.subtract)\
                   .then_inc(S["xlo_ready"], 1)

            def landed(k):
                dve.wait_ge(S["x_landed"], 16 * (k + 1))

            def hidden(k):
                dve.wait_ge(S["silu_ready"], k + 1)
                dve.tensor_tensor(sh[:, :], z_ps[:, :], sh[:, :], ALU.mult).then_inc(S["h_ready"], 1)

            def h_lo(k):
                dve.wait_ge(S["hhi_ready"], k + 1)
                dve.tensor_tensor(hpart(1), ht_ps[:, :], hpart(0).bitcast(F32), ALU.subtract)\
                   .then_inc(S["hlo_ready"], 1)

            def update(k):
                at = ring_slot(k)
                dve.wait_ge(S["y_done"], k + 1)
                dve.scalar_tensor_tensor(out=rows[:, ds(at, 1), :], in0=y_ps[:, :].unsqueeze(1),
                                         scalar=tg[:, 0:1], in1=rows[:, ds(at, 1), :],
                                         op0=ALU.mult, op1=ALU.add).then_inc(S["rows_ready"], 1)

            def piece_lo(q):
                dve.wait_ge(S["piece_hi"], q + 1)
                at = ds(q % 2 * PIECE, PIECE)
                dve.tensor_tensor(wgu[:, ds(q // 2, 1), 1, at], raw[:, ds(q % RAWS, 1), :],
                                  wgu[:, ds(q // 2, 1), 0, at].bitcast(F32), ALU.subtract)\
                   .then_inc(S["piece_lo"], 1)

            def check(c):
                dve.wait_ge(S["check_landed"], 16 * (c + 1))
                dve.wait_ge(S["bits_done"], c + 1)
                dve.scalar_tensor_tensor(out=low_bits.unsqueeze(1), in0=checked[:, ds(c % 2, 1), :],
                                         scalar=LO_BITS, in1=low_bits.unsqueeze(1),
                                         op0=ALU.bitwise_and, op1=ALU.bitwise_or)\
                   .then_inc(S["bits_done"], 1)

            def step(k):
                h_lo(k - 1)
                norm(k + 1, ring_slot(k + 1))
                landed(k + 2)
                stats(k + 2, ring_slot(k + 2))
                piece_lo(k - 1)
                hidden(k)
                x_lo(k + 1, 0, 0)
                update(k - 1)

            for n in range(5):
                ctx_lo(n)
            landed(0)
            stats(0, ring_slot(0))
            ctx_lo(5)
            norm(0, ring_slot(0))
            for n in range(6, 9):
                ctx_lo(n)
            x_lo(0, 0, 0)
            for n in range(9, EXPERTS * KC):
                ctx_lo(n)
            landed(1)
            stats(1, ring_slot(1))
            norm(1, ring_slot(1))
            landed(2)
            stats(2, ring_slot(2))
            dve.tensor_tensor(is_low[1][:, :, :], per(low[:, 1, :], P), across(P), ALU.is_equal)
            then(dve.tensor_tensor(is_high2[:, :, :], per(high[:, 1, :], TILES), across(TILES),
                                   ALU.is_equal))
            dve.tensor_tensor(is_high2[:, :, :], is_high2[:, :, :], per(token[:, :], TILES), ALU.mult)\
               .then_inc(S["route_sb"], 1)
            hidden(0)
            x_lo(1, 0, 0)
            dve.wait_ge(S["gates_ready"], 1)
            dve.tensor_scalar(dsb[:, :], dsb[:, :], tg[:, 1:2], None, ALU.mult).then_inc(S["dsb_ready"], 1)
            dve.wait_ge(S["route_pe"], 3)
            dve.tensor_copy(oidx[:, :], bank[4][:, 0:TILES]).then_inc(S["oidx_ready"], 1)
            with dve.Fori(1, IC + 1) as k:
                step(k)
                check(k - 1)
            with dve.Fori(IC + 1, PIECES + 1) as k:
                step(k)
            h_lo(16)
            norm(18, ring_slot(18))
            dve.wait_ge(S["rows_a"], 16)
            stats(19, row_slot(0, 0))
            hidden(17)
            x_lo(18, 0, 0)
            update(16)
            dve.wait_ge(S["sums_done"], PIECES)
            dve.tensor_reduce(loose[:, 0:1], lo_sums[:, :], AX, ALU.add)
            dve.wait_ge(S["bits_done"], IC + 1)
            dve.tensor_reduce(loose[:, 1:2], low_bits, AX, ALU.max).then_inc(S["loose_step"], 1)
            dve.wait_ge(S["loose_step"], 1)
            dve.tensor_tensor(loose[:, 2:3], loose[:, 0:1], loose[:, 1:2], ALU.add)\
               .then_inc(S["loose_step"], 1)
            dve.wait_ge(S["loose_step"], 2)
            dve.tensor_scalar(loose[:, 3:4], loose[:, 2:3], 0.0, None, ALU.not_equal)\
               .then_inc(S["loose_ready"], 1)
            h_lo(17)
            norm(19, row_slot(0, 0))
            stats(20, row_slot(0, 1))
            x_lo(19, 0, 2)
            dve.wait_ge(S["loose_counted"], 1)
            dve.tensor_scalar(flag[:, :], bank[2][0:1, 0:1], 0.0, None, ALU.is_lt)\
               .then_inc(S["flag_ready"], 1)
            hidden(18)
            update(17)
            norm(20, row_slot(0, 1))
            dve.wait_ge(S["rows_b"], 16)
            stats(21, row_slot(0, 2))
            h_lo(18)
            x_lo(20, 0, 3)
            norm(21, row_slot(0, 2))
            stats(22, row_slot(0, 3))
            x_lo(21, 0, 0)
            norm(22, row_slot(0, 3))
            update(18)
            x_lo(22, 0, 1)

            def down_lo(c):
                dve.wait_ge(S["down_hi"], c + 1)
                dve.tensor_tensor(down_w(c, 1), rows[:, 2 + c % 4, :], down_w(c, 0).bitcast(F32),
                                  ALU.subtract).then_inc(S["down_lo"], 1)

            def chunk(b, c):
                n = STEPS + IC * b + c
                dve.wait_ge(S["silu_ready"], n + 1)
                dve.wait_ge(S["u_done"], n - STEPS + 1)
                dve.scalar_tensor_tensor(out=sh[:, :], in0=u_ps[:, :], scalar=gs[:, 1, c:c + 1],
                                         in1=sh[:, :], op0=ALU.mult, op1=ALU.mult)\
                   .then_inc(S["h_ready"], 1)
                dve.wait_ge(S["hhi_ready"], n + 1)
                dve.tensor_tensor(hslot(c)[:, 1, :], sh[:, :],
                                  hslot(c)[:, 0, :].bitcast(F32), ALU.subtract)\
                   .then_inc(S["hlo_ready"], 1)

            def prepare(b, t):
                m = STEPS + BLOCK * b + t
                at = row_slot(b, t)
                if t == 0:
                    dve.wait_ge(S["rows_a"], 16 * (b + 1))
                if t == 2:
                    dve.wait_ge(S["rows_b"], 16 * (b + 1))
                stats(m, at)
                norm(m, at)

            def scale(b, u):
                n = BLOCK * b + u
                buf = (tmp, xn)[u % 2]
                dve.wait_ge(S["acc_done"], n + 1)
                if u >= 2:
                    dve.wait_ge(S["rows_ready"], STEPS + n - 1)
                dve.tensor_tensor(buf[:, :].unsqueeze(1), acc_ps[u][:, :].unsqueeze(1),
                                  dsb[:, :].unsqueeze(1), ALU.mult).then_inc(S["scaled"], 1)

            def add(b, u):
                at = row_slot(b, (u + 2) % BLOCK)
                dve.wait_ge(S["scaled"], BLOCK * (b + 1) + u + 1)
                dve.tensor_tensor(rows[:, ds(at, 1), :], rows[:, ds(at, 1), :],
                                  (tmp, xn)[u % 2][:, :].unsqueeze(1), ALU.add)\
                   .then_inc(S["rows_ready"], 1)

            def finish(b):
                dve.wait_ge(S["rows_ready"], STEPS + BLOCK * b)
                for u in range(0, BLOCK, 2):
                    scale(b, u)
                    scale(b, u + 1)
                    add(b, u)
                    add(b, u + 1)

            def mlp_block(b, first=False, last=False):
                for c in range(IC):
                    chunk(b, c)
                    if first:
                        for d in range(3 * c, min(3 * c + 3, IC)):
                            down_lo(d)
                    if c == 0 and not first:
                        dve.wait_ge(S["xt_done"], STEPS + BLOCK * (b + 1))
                        finish(b - 1)
                    if c - 1 in PREP_AT and not last:
                        t = PREP_AT[c - 1]
                        x_lo(STEPS + BLOCK * (b + 1) + t, b + 1, (t + 2) % BLOCK)
                    if c in PREP_AT and not last:
                        if PREP_AT[c] == 0:
                            dve.wait_ge(S["rows_ready"], STEPS + BLOCK * b)
                        prepare(b + 1, PREP_AT[c])

            dve.sem_inc(S["scaled"], BLOCK)
            mlp_block(0, first=True)
            with dve.Fori(1, BLOCKS - 1) as b:
                mlp_block(b)
            mlp_block(BLOCKS - 1, last=True)
            finish(BLOCKS - 1)

        @block.tensor
        def _(pe):
            pe.wait_ge(S["consts"], 9)
            pe.wait_ge(S["route_sb"], 1)
            pe.matmul(bank[2][:, 0:EXPERTS], tri[:, :], here16[:, :], start=True, stop=True)
            pe.matmul(bank[2][:, EXPERTS:2 * EXPERTS], ones16[:, :], here16[:, :], start=True, stop=True)\
              .then_inc(S["route_pe"], 1)
            pe.wait_ge(S["route_sb"], 2)
            for c in range(CT):
                mm = pe.matmul(bank[3][:, 0:3 * STEPS], is_low[0][:, c, :],
                               is_high[:, c, :, :].rearrange("p a k -> p (a k)"),
                               start=c == 0, stop=c == CT - 1)
            mm.then_inc(S["route_pe"], 1)

            def turn_x(m):
                pe.wait_ge(S["xn_ready"], m + 1)
                if not isinstance(m, int) or m:
                    pe.wait_ge(S["xlo_ready"], m)
                for c in range(KC):
                    mm = pe.transpose(xt_ps[:, c * P:(c + 1) * P], xn[:, c * P:(c + 1) * P], ident[:, :])
                mm.then_inc(S["xt_done"], 1)

            def expert_product(out_ps, part, e):
                last = len(PASSES) * KC - 1
                for n in range(last + 1):
                    (s, w), c = PASSES[n // KC], n % KC
                    mm = pe.matmul(out_ps[:, :], part(s)[:, c * P:(c + 1) * P], ctx_w(e, c, w),
                                   start=n == 0, stop=n == last)
                return mm

            def expert(k):
                return pe.value_load(eidx[0:1, ds(k, 1)], min_val=0, max_val=EXPERTS - 1)

            def first_product(k):
                pe.wait_ge(S["xlo_ready"], k + 1)
                expert_product(z_ps, lambda s: xpart(0, 0, s), expert(k)).then_inc(S["z_done"], 1)

            def turn_h(k):
                pe.wait_ge(S["h_ready"], k + 1)
                for c in range(KC):
                    mm = pe.transpose(ht_ps[:, c * P:(c + 1) * P], sh[:, c * P:(c + 1) * P], ident[:, :])
                mm.then_inc(S["ht_done"], 1)

            def second_product(k):
                pe.wait_ge(S["hlo_ready"], k + 1)
                if not isinstance(k, int) or k:
                    pe.wait_ge(S["rows_ready"], k)
                expert_product(y_ps, hpart, expert(k)).then_inc(S["y_done"], 1)

            turn_x(0)
            pe.wait_ge(S["tables_ready"], 1)
            pe.wait_ge(S["ctx_lo"], EXPERTS * KC)
            first_product(0)
            turn_x(1)
            pe.wait_ge(S["route_sb"], 3)
            for c in range(CT):
                mm = pe.matmul(bank[4][:, 0:TILES], is_low[1][:, c, :], is_high2[:, c, :],
                               start=c == 0, stop=c == CT - 1)
            mm.then_inc(S["route_pe"], 1)
            turn_h(0)
            with pe.Fori(1, PIECES + 1) as k:
                first_product(k)
                turn_x(k + 1)
                second_product(k - 1)
                turn_h(k)
            first_product(17)
            turn_x(18)
            second_product(16)
            turn_h(17)
            first_product(18)
            turn_x(19)
            pe.wait_ge(S["loose_ready"], 1)
            pe.matmul(bank[2][0:1, 0:1], loose[:, 3:4], half[:, :], start=True, stop=True)\
              .then_inc(S["loose_counted"], 1)
            second_product(17)
            turn_h(18)
            turn_x(20)
            turn_x(21)
            second_product(18)
            turn_x(22)

            def inner_product(out_ps, b, row, c, passes):
                last = len(passes) * KC - 1
                for n in range(last + 1):
                    (w, s), h = passes[n // KC], n % KC
                    moving = xbuf(b).rearrange("p (u s h j) -> p s h u j", u=BLOCK, s=2, h=KC)[:, s, h]
                    mm = pe.matmul(out_ps[:, :], wgu[:, row + h, w, c * P:(c + 1) * P], moving,
                                   start=n == 0, stop=n == last)
                return mm

            def down_product(b, c, passes):
                pe.wait_ge(S["hlo_ready"], STEPS + IC * b + c + 1)
                pe.wait_ge(S["down_lo"], c + 1)
                for u in range(BLOCK):
                    if c == 0:
                        pe.wait_ge(S["scaled"], BLOCK * b + u + 1)
                    for n, (w, s) in enumerate(passes):
                        mm = pe.matmul(acc_ps[u][:, :], hslot(c)[:, s, u * P:(u + 1) * P],
                                       down_w(c, w), start=c == 0 and n == 0,
                                       stop=c == IC - 1 and n == len(passes) - 1)
                    if c == IC - 1:
                        mm.then_inc(S["acc_done"], 1)

            def second_mlp(passes):
                with pe.Fori(0, BLOCKS) as b:
                    pe.wait_ge(S["xlo_ready"], STEPS + BLOCK * (b + 1))
                    for c in range(IC):
                        n = STEPS + IC * b + c
                        pe.wait_ge(S["silu_ready"], n)
                        inner_product(g_ps, b, 0, c, passes).then_inc(S["z_done"], 1)
                        pe.wait_ge(S["h_ready"], n)
                        inner_product(u_ps, b, KC, c, passes).then_inc(S["u_done"], 1)
                        if c - 1 in PREP_AT:
                            with pe.If(b < BLOCKS - 1):
                                turn_x(STEPS + BLOCK * (b + 1) + PREP_AT[c - 1])
                        if c:
                            down_product(b, c - 1, passes)
                        else:
                            with pe.If(b > 0):
                                down_product(b - 1, IC - 1, passes)
                down_product(BLOCKS - 1, IC - 1, passes)

            pe.wait_ge(S["flag_ready"], 1)
            pe.wait_ge(S["rows_ready"], STEPS)
            has_lo = pe.value_load(flag[0:1, 0:1], min_val=0, max_val=1)
            with pe.If(has_lo > 0):
                second_mlp([(0, 0), (1, 0), (0, 1)])
            with pe.Else():
                second_mlp([(0, 0), (0, 1)])


def kernel(x, itok_BxS_13_99985, ctx_2048, g_xattn, g_ffn, L0_ffn_gate_w, L0_ffn_up_w,
           L0_ffn_down_w, L0_ffn_gate_s, L0_ffn_up_s, L0_ffn_down_s):
    import numpy as np
    import concourse.bacc as bacc
    from concourse.bass_utils import run_bass_kernel_spmd

    x, ids, ctx, gate, up, down = (np.asarray(a) for a in (
        x, itok_BxS_13_99985, ctx_2048, L0_ffn_gate_w, L0_ffn_up_w, L0_ffn_down_w))
    arrays = {
        "x": np.ascontiguousarray(x.reshape(TOKENS, D)),
        "ids": np.ascontiguousarray(ids.reshape(P, CT)),
        "ctxT": np.ascontiguousarray(ctx.transpose(0, 2, 1)),
        "g_x": np.asarray(g_xattn),
        "g_f": np.asarray(g_ffn),
        "guT": np.ascontiguousarray(np.concatenate([gate.T, up.T])),
        "dwT": np.ascontiguousarray(down.T),
        "gate_s": np.ascontiguousarray(np.asarray(L0_ffn_gate_s).reshape(IC, P).T),
        "up_s": np.ascontiguousarray(np.asarray(L0_ffn_up_s).reshape(IC, P).T),
        "down_s": np.asarray(L0_ffn_down_s),
    }
    nc = bacc.Bacc("TRN2", target_bir_lowering=False, num_devices=1)
    args = [nc.dram_tensor(n, a.shape, mybir.dt.from_np(a.dtype), kind="ExternalInput").ap()
            for n, a in arrays.items()]
    out = nc.dram_tensor("out", (TOKENS, D), F32, kind="ExternalOutput").ap()
    build(nc, *args, out)
    r = run_bass_kernel_spmd(nc, [arrays], core_ids=[0])
    return r.results[0]["out"].reshape(4, TOKENS // 4, D)
```

```python
from contextlib import ExitStack

import concourse.bass as bass
from concourse import mybir
from concourse.bass import ds

F32 = mybir.dt.float32
F32R = mybir.dt.float32r
FP16 = mybir.dt.float16
I32 = mybir.dt.int32
U32 = mybir.dt.uint32
ALU = mybir.AluOpType
ACT = mybir.ActivationFunctionType
AX = mybir.AxisListType.X

P = 128
TOKENS = 2048
D = 512
KC = D // P
EXPERTS = 4
VOCAB = 25000
PER_EXPERT = VOCAB // EXPERTS
TILES = TOKENS // P
STEPS = TILES + EXPERTS - 1
CT = TOKENS // P
INTER = 1408
IC = INTER // P
BLOCK = 4
BLOCKS = TILES // BLOCK
PIECE = INTER // 2
PIECES = 2 * KC * 2
RING = 6
ROWS = 8
POOL_LO = 5
POOL_LO_NEXT = 7
POOL_LO_LATE = 14
PACKED = 15
RAWS = 4
EPS = 1e-5
LO_BITS = (1 << 12) - 1
PASSES = [(0, 0), (1, 0), (0, 1)]
CTX_WORDS = EXPERTS * KC * 2 * D
XBUF_WORDS = BLOCK * 2 * D
PREP_AT = {5: 0, 6: 1, 7: 2, 8: 3}


def ring_slot(k):
    return (k + 4) % RING


def row_slot(b, t):
    return (RING + BLOCK * b + t) % ROWS


def down_slot(c):
    return 2 + (c + 3) % 4


def build(nc, x, ids, ctxT, g_x, g_f, guT, dwT, gate_s, up_s, down_s, out):
    scratch = nc.dram_tensor("x1_rows", [2 * TOKENS + STEPS * P, D], F32).ap()
    ctx_v = ctxT.rearrange("e (c p) f -> e p c f", p=P)
    gu_v = guT.rearrange("(r p) (v n) -> p r v n", p=P, v=2)
    dw_v = dwT.rearrange("(c p) h -> c p h", p=P)
    x1_v = scratch[0:TOKENS, :].rearrange("(t p) h -> p t h", p=P)

    with ExitStack() as ctx:
        def sb(name, shape, dt):
            return ctx.enter_context(nc.sbuf_tensor(name, shape, dt))

        def psum(name):
            return ctx.enter_context(nc.psum_tensor(name, [P, D], F32))

        def sem(name):
            return ctx.enter_context(nc.semaphore(name))

        work_base = (nc.sbuf_base + 31) // 32 * 32
        work = sb("work", [P, CTX_WORDS + XBUF_WORDS], F32R)
        wgu_base = nc.sbuf_base
        wgu = sb("wgu", [P, 2 * KC, 2, INTER], F32R)
        raw_base = nc.sbuf_base
        raw = sb("raw", [P, RAWS, PIECE], F32)
        rows = sb("rows", [P, ROWS, D], F32)
        xn = sb("xn", [P, D], F32)
        sh = sb("sh", [P, D], F32)
        tmp = sb("tmp", [P, D], F32)
        dsb = sb("dsb", [P, D], F32)
        ident = sb("ident", [P, P], F32)
        bn = sb("bn", [P, 2, 6], F32)
        mv = sb("mv", [P, 1 + BLOCK, 2], F32)
        ve = sb("ve", [P, 1 + BLOCK], F32)
        rstd = sb("rstd", [P, 1 + BLOCK], F32)
        half = sb("half", [P, 1], F32)
        gs = sb("gs", [P, 2, IC], F32)
        lo_sums = sb("lo_sums", [P, PIECES], F32)
        loose = sb("loose", [P, 4], F32)
        flag = sb("flag", [1, 1], I32)
        gg = sb("gg", [P, 2], F32)
        tg = sb("tg", [P, 2], F32)
        gidx = sb("gidx", [P, STEPS], U32)
        sidx = sb("sidx", [P, STEPS], U32)
        oidx = sb("oidx", [P, TILES], U32)
        tiles = sb("tiles", [1, 2, STEPS], I32)
        inow = sb("inow", [P, 2], U32)


        hp = [nc.alloc_sbuf_tensor_at(f"hp{n}", [P, 2, D], F32R, offset=at) for n, at in enumerate(
            (raw_base, raw_base + 2 * D * 4, work_base + IC * 2 * D * 4))]
        spare = work_base + (CTX_WORDS + XBUF_WORDS // 2) * 4
        checked = nc.alloc_sbuf_tensor_at("checked", [P, 2, D], I32, offset=spare)
        junk = nc.alloc_sbuf_tensor_at("junk", [P, PIECE], F32, offset=spare + 2 * D * 4)
        low_bits = tmp[:, :].bitcast(I32)
        wgu_bytes = 2 * KC * 2 * INTER * 4
        ctx_in_bytes = EXPERTS * KC * D * 4
        ctx_in = nc.alloc_sbuf_tensor_at("ctx_in", [P, EXPERTS, KC, D], F32,
                                         offset=wgu_base + wgu_bytes - ctx_in_bytes)
        route_at = [wgu_base + 3 * 2 * INTER * 4]

        def rt(name, shape, dt):
            count = 1
            for n in shape[1:]:
                count *= n
            at = route_at[0]
            route_at[0] = (at + count * (2 if dt == FP16 else 4) + 31) // 32 * 32
            assert route_at[0] <= wgu_base + wgu_bytes - ctx_in_bytes
            return nc.alloc_sbuf_tensor_at(name, shape, dt, offset=at)

        ids_i = rt("ids_i", [P, CT], I32)
        ids_f = rt("ids_f", [P, CT], F32)
        at_least = rt("at_least", [P, EXPERTS + 1, CT], F32)
        of = rt("of", [P, EXPERTS, CT], F32)
        ones_f = rt("ones_f", [P, EXPERTS * CT], F32)
        seen = rt("seen", [P, EXPERTS, CT], F32)
        here = rt("here", [P, EXPERTS], F32)
        here16 = rt("here16", [P, EXPERTS], FP16)
        tri = rt("tri", [P, P], FP16)
        ones16 = rt("ones16", [P, P], FP16)
        before = rt("before", [P, 2, EXPERTS], F32)
        pad_i = rt("pad_i", [P, EXPERTS], I32)
        pad = rt("pad", [P, EXPERTS], F32)
        pad_end = rt("pad_end", [P, EXPERTS], F32)
        end = rt("end", [P, EXPERTS], F32)
        small = [rt(f"small{n}", [P, EXPERTS], F32) for n in range(6)]
        pos = [rt(f"pos{n}", [P, EXPERTS, CT], F32) for n in range(3)]
        slot = rt("slot", [P, CT], F32)
        shift = rt("shift", [P, CT], F32)
        rank = rt("rank", [P, CT], F32)
        place_i = rt("place_i", [P, 2, CT], I32)
        low_i = rt("low_i", [P, 2, CT], I32)
        high_i = rt("high_i", [P, 2, CT], I32)
        low = rt("low", [P, 2, CT], F32)
        high = rt("high", [P, 2, CT], F32)
        iota_p = rt("iota_p", [P, P], F32)
        token = rt("token", [P, CT], F32)
        dump = rt("dump", [P, STEPS], F32)
        tile_at = rt("tile_at", [1, STEPS], F32)
        is_low = [rt(f"is_low{n}", [P, CT, P], FP16) for n in range(2)]
        is_high = rt("is_high", [P, CT, 3, STEPS], FP16)
        is_high2 = rt("is_high2", [P, CT, TILES], FP16)
        table = rt("table", [P, 3, STEPS], F32)
        empty = rt("empty", [P, 2, STEPS], F32)
        owner = rt("owner", [1, 4, STEPS], F32)
        shifts = rt("shifts", [1, PACKED], I32)
        shifted = rt("shifted", [1, 2, PACKED], I32)
        packed = rt("packed", [1, 2], I32)

        bank = [psum(f"bank{n}") for n in range(8)]
        z_ps, y_ps, g_ps, u_ps = bank[0], bank[1], bank[0], bank[1]
        acc_ps = bank[2:6]
        xt_ps, ht_ps = bank[6], bank[7]

        def hslot(c):
            return hp[2 if c == IC - 1 else c % 2]

        def halves(b, c):
            if isinstance(b, int) and (b, c) == (BLOCKS - 1, IC - 1):
                return slice(0, D // 2), slice(D // 2, D)
            return slice(0, D),

        def xbuf(b):
            base = CTX_WORDS - XBUF_WORDS * (b % 2)
            return work[:, ds(base, XBUF_WORDS)]

        def xpart(b, u, s):
            base = CTX_WORDS - XBUF_WORDS * (b % 2)
            return work[:, ds(base + (2 * u + s) * D, D)]

        def hpart(s, last=False):
            if last:
                return hp[0][:, s, :]
            return work[:, CTX_WORDS + (2 + s) * D:CTX_WORDS + (3 + s) * D]

        def ctx_w(e, c, s):
            return work[:, ds(e * (KC * 2 * D) + (c * 2 + s) * D, D)]

        def down_w(c, s):
            return work[:, (c * 2 + s) * D:(c * 2 + s + 1) * D]

        names = """ids_in small_in consts route_pe route_sb route_step tables_ready
            piece_landed piece_hi piece_lo down_hi down_lo x_landed stored rows_a rows_b
            bn_parts bn_mv var_ready rstd_ready xn_ready xt_done xhi_ready xlo_ready
            z_done y_done silu_ready h_ready ht_done hhi_ready hlo_ready u_done rows_ready
            scaled gates_ready dsb_ready ctx_hi ctx_lo out_stored index_now held
            check_landed bits_done sums_done loose_step loose_ready loose_counted flag_ready
            acc_done oidx_ready table_loaded""".split()
        S = {n: sem(n) for n in names}
        ctx_landed = [sem(f"ctx_landed{e}") for e in range(EXPERTS)]
        down_landed = [sem(f"down_landed{n}") for n in range(4)]
        last_stored = [sem(f"last_stored{t}") for t in range(BLOCK)]

        def hold(eng):
            eng.sem_inc(S["held"])

        def ctx_lo(eng, n):
            eng.wait_ge(S["ctx_hi"], n + 1)
            eng.tensor_tensor(ctx_w(n // KC, n % KC, 1), ctx_in[:, n // KC, n % KC, :],
                              ctx_w(n // KC, n % KC, 0).bitcast(F32), ALU.subtract)\
               .then_inc(S["ctx_lo"], 1)

        block = ctx.enter_context(nc.Block())

        @block.sync
        def _(sp):
            sp.dma_start(ids_i[:, :], ids).then_inc(S["ids_in"], 16)
            for e in range(EXPERTS):
                sp.dma_start(ctx_in[:, e], ctx_v[e]).then_inc(ctx_landed[e], 16)
            sp.wait_ge(S["x_landed"], 16)
            for s, src in enumerate((gate_s, up_s)):
                sp.dma_start(gs[:, s, :], src).then_inc(S["small_in"], 16)
            sp.wait_ge(S["table_loaded"], 1)
            for s, src in enumerate((g_x, g_f)):
                sp.dma_start(gg[:, s:s + 1], src.partition_broadcast(P)).then_inc(S["small_in"], 16)
            sp.dma_start(dsb[:, :], down_s.partition_broadcast(P)).then_inc(S["small_in"], 16)

            def piece_at(q):
                return sp.snap(q % RAWS), sp.snap(q // 2), sp.snap(q % 2), sp.snap(q - RAWS + 1), sp.snap(16 * q)

            def piece(at, row, half_):
                sp.dma_start(raw[:, ds(at, 1), :], gu_v[:, ds(row, 1), ds(half_, 1), :])\
                  .then_inc(S["piece_landed"], 16)

            for q in range(RAWS):
                if q:
                    sp.wait_ge(S["piece_landed"], 16 * q)
                piece(q % RAWS, q // 2, q % 2)

            def check_row(c):
                sp.dma_start(checked[:, ds(c % 2, 1), :], dw_v[ds(c, 1)].bitcast(I32)
                             .rearrange("c p h -> p c h")).then_inc(S["check_landed"], 16)

            check_row(0)
            sp.wait_ge(S["check_landed"], 16)
            check_row(1)

            def next_piece(q):
                *at, split, all_before = piece_at(q)
                sp.wait_ge(S["piece_landed"], all_before)
                hold(sp)
                sp.wait_ge(S["piece_lo"], split)
                hold(sp)
                piece(*at)

            with sp.Fori(RAWS, RAWS + IC - 2) as q:
                next_piece(q)
                c, c_before, c_checked = sp.snap(q - 2), sp.snap(16 * (q - 2)), sp.snap(q - 2)
                sp.wait_ge(S["check_landed"], c_before)
                hold(sp)
                sp.wait_ge(S["bits_done"], c_checked)
                hold(sp)
                check_row(c)
            with sp.Fori(RAWS + IC - 2, PIECES) as q:
                next_piece(q)

            def load_rows(b):
                for half_, landed in enumerate((S["rows_a"], S["rows_b"])):
                    t = BLOCK * b + 2 * half_
                    at = row_slot(b, 2 * half_)
                    sp.dma_start(rows[:, at:at + 2, :], x1_v[:, t:t + 2, :]).then_inc(landed, 16)
                    if b == 0 and half_ == 0:
                        sp.wait_ge(S["stored"], 16 * 16)

            sp.wait_ge(S["stored"], 16 * (BLOCK + EXPERTS - 1))
            load_rows(0)
            for c in range(IC):
                if c < 4:
                    sp.wait_ge(S["stored"], 16 * (TILES + c))
                else:
                    sp.wait_ge(S["down_lo"], c - 3)
                sp.dma_start(rows[:, down_slot(c), :], dw_v[c]).then_inc(down_landed[c % 4], 16)
            sp.wait_ge(S["down_lo"], IC)
            load_rows(1)
            for b in range(2, BLOCKS):
                sp.wait_ge(S["out_stored"], 16 * BLOCK * (b - 1))
                load_rows(b)
            sp.wait_ge(S["out_stored"], 16 * BLOCK * (BLOCKS - 1))
            for t in range(BLOCK):
                sp.wait_ge(last_stored[t], 16)

        @block.gpsimd
        def _(pool):
            pool.memset(half[:, :], -0.5).then_inc(S["consts"], 1)
            pool.memset(ident[:, :], 0.0).then_inc(S["consts"], 1)
            pool.memset(ones16[:, :], 1.0).then_inc(S["consts"], 1)
            pool.wait_ge(S["consts"], 3)
            pool.affine_select(out=ident[:, :], in_=ident[:, :], compare_op=ALU.not_equal, fill=1.0,
                               base=0, pattern=[[-1, P]], channel_multiplier=1).then_inc(S["consts"], 1)
            pool.affine_select(out=tri[:, :], in_=ones16[:, :], compare_op=ALU.is_gt, fill=0.0,
                               base=0, pattern=[[1, P]], channel_multiplier=-1).then_inc(S["consts"], 1)
            exact = dict(allow_small_or_imprecise_dtypes=True)
            pool.iota(iota_p[:, :], pattern=[[1, P]], base=0, channel_multiplier=0, **exact)\
                .then_inc(S["consts"], 1)
            pool.iota(token[:, :], pattern=[[1, CT]], base=0, channel_multiplier=CT, **exact)\
                .then_inc(S["consts"], 1)
            pool.iota(dump[:, :], pattern=[[P, STEPS]], base=TOKENS, channel_multiplier=1, **exact)\
                .then_inc(S["consts"], 1)
            pool.iota(tile_at[:, :], pattern=[[P, STEPS]], base=0, channel_multiplier=0, **exact)\
                .then_inc(S["consts"], 1)
            pool.iota(shifts[:, :], pattern=[[2, PACKED]], base=0, channel_multiplier=0)\
                .then_inc(S["consts"], 1)
            pool.wait_ge(S["consts"], 10)

            def gather(at, index):
                pool.indirect_dma_start(
                    rows[:, at, :], None, x, bass.IndirectOffsetOnAxis(ap=index, axis=0))\
                    .then_inc(S["x_landed"], 16)

            def store(at, index):
                pool.indirect_dma_start(
                    scratch, bass.IndirectOffsetOnAxis(ap=index, axis=0), rows[:, at, :], None)\
                    .then_inc(S["stored"], 16)

            def inverse_std(m):
                pool.wait_ge(S["var_ready"], m + 1)
                pool.tensor_tensor(rstd[:, 0:1], ve[:, 0:1], half[:, :], ALU.pow)\
                    .then_inc(S["rstd_ready"], 1)

            def first_inverse_std(t):
                pool.wait_ge(S["var_ready"], STEPS + t + 2)
                pool.tensor_tensor(rstd[:, 1 + t:3 + t], ve[:, 1 + t:3 + t],
                                   half[:, :].to_broadcast([P, 2]), ALU.pow).then_inc(S["rstd_ready"], 2)

            pool.memset(low_bits, 0).then_inc(S["bits_done"], 1)
            for n in range(POOL_LO):
                ctx_lo(pool, n)

            pool.wait_ge(S["tables_ready"], 1)
            for k in range(5):
                if k:
                    pool.wait_ge(S["x_landed"], 16 * k)
                gather(ring_slot(k), gidx[:, k:k + 1])
                if k == 0:
                    for n in range(POOL_LO, POOL_LO_NEXT):
                        ctx_lo(pool, n)
                if k == 1:
                    inverse_std(0)
                if k == 2:
                    for n in range(POOL_LO_LATE, EXPERTS * KC):
                        ctx_lo(pool, n)
                    inverse_std(1)
            inverse_std(2)
            inverse_std(3)
            pool.wait_ge(S["x_landed"], 16 * 5)
            gather(ring_slot(5), gidx[:, 5:6])
            pool.wait_ge(S["tables_ready"], 2)
            pool.wait_ge(S["rows_ready"], 1)
            store(ring_slot(0), sidx[:, 0:1])

            with pool.Fori(0, 2) as i:
                for j in range(RING):
                    k = 2 + RING * i + j
                    inverse_std(k + 2)
                    pool.wait_ge(S["x_landed"], 16 * (k + 4))
                    pool.tensor_copy(inow[:, 0:1], gidx[:, ds(k + 4, 1)]).then_inc(S["index_now"], 1)
                    pool.wait_ge(S["stored"], 16 * (k - 1))
                    pool.tensor_copy(inow[:, 1:2], sidx[:, ds(k - 1, 1)]).then_inc(S["index_now"], 1)
                    pool.wait_ge(S["index_now"], 2 * (k - 1))
                    hold(pool)
                    gather(ring_slot(2 + j + 4), inow[:, 0:1])
                    pool.wait_ge(S["rows_ready"], k)
                    hold(pool)
                    store(ring_slot(2 + j - 1), inow[:, 1:2])
            for k in range(14, STEPS + 1):
                if k + 2 < STEPS:
                    inverse_std(k + 2)
                elif k < STEPS:
                    first_inverse_std(2 * (k + 2 - STEPS))
                if k + 4 < STEPS:
                    pool.wait_ge(S["stored"], 16 * (k - 1))
                    pool.wait_ge(S["x_landed"], 16 * (k + 4))
                    gather(ring_slot(k + 4), gidx[:, k + 4:k + 5])
                pool.wait_ge(S["stored"], 16 * (k - 1))
                pool.wait_ge(S["rows_ready"], k)
                store(ring_slot(k - 1), sidx[:, k - 1:k])

            pool.wait_ge(S["oidx_ready"], 1)
            for b in range(BLOCKS):
                if b + 1 < BLOCKS:
                    for t in range(BLOCK):
                        inverse_std(STEPS + BLOCK * (b + 1) + t)
                for u in range(BLOCK):
                    n, t = BLOCK * b + u, (u + 2) % BLOCK
                    pool.wait_ge(S["rows_ready"], STEPS + n + 1)
                    if b + 1 < BLOCKS:
                        if n:
                            pool.wait_ge(S["out_stored"], 16 * n)
                        done = S["out_stored"]
                    else:
                        done = last_stored[t]
                    pool.indirect_dma_start(
                        out, bass.IndirectOffsetOnAxis(ap=oidx[:, BLOCK * b + t:BLOCK * b + t + 1], axis=0),
                        rows[:, row_slot(b, t), :], None).then_inc(done, 16)

        @block.scalar
        def _(act):
            act.wait_ge(S["consts"], 1)
            act.activation(gg[:, 0:1], half[:, :], ACT.Silu).then_inc(S["table_loaded"], 1)
            for e in range(EXPERTS):
                act.wait_ge(ctx_landed[e], 16)
                for c in range(KC):
                    act.activation(ctx_w(e, c, 0), ctx_in[:, e, c, :], ACT.Copy).then_inc(S["ctx_hi"], 1)
            act.wait_ge(S["small_in"], 16 * 5)
            act.activation(tg[:, :], gg[:, :], ACT.Tanh).then_inc(S["gates_ready"], 1)

            def x_hi(m, b, u, turned=xt_ps):
                act.wait_ge(S["xt_done"], m + 1)
                act.activation(xpart(b, u, 0), turned[:, :], ACT.Copy).then_inc(S["xhi_ready"], 1)

            def h_hi(k, last=False):
                act.wait_ge(S["ht_done"], k + 1)
                act.activation(hpart(0, last), ht_ps[:, :], ACT.Copy).then_inc(S["hhi_ready"], 1)

            def silu(k):
                act.wait_ge(S["z_done"], k + 1)
                act.activation(sh[:, :], z_ps[:, :], ACT.Silu).then_inc(S["silu_ready"], 1)

            def piece_hi(q):
                act.wait_ge(S["piece_landed"], 16 * (q + 1))
                act.activation(wgu[:, ds(q // 2, 1), 0, ds(q % 2 * PIECE, PIECE)],
                               raw[:, ds(q % RAWS, 1), :], ACT.Copy).then_inc(S["piece_hi"], 1)

            def piece_sum(q):
                act.wait_ge(S["piece_lo"], q + 1)
                act.activation(junk[:, :], wgu[:, ds(q // 2, 1), 1, ds(q % 2 * PIECE, PIECE)].bitcast(F32),
                               ACT.Abs, accum_out=lo_sums[:, ds(q, 1)]).then_inc(S["sums_done"], 1)

            x_hi(0, 0, 0)
            silu(0)
            x_hi(1, 0, 0)
            with act.Fori(1, PIECES + 1) as k:
                h_hi(k - 1)
                piece_hi(k - 1)
                silu(k)
                x_hi(k + 1, 0, 0)
                piece_sum(k - 1)
            h_hi(16)
            silu(17)
            x_hi(18, 0, 0)
            h_hi(17)
            x_hi(19, 0, 2, bank[2])
            x_hi(20, 0, 3, bank[3])
            silu(18)
            x_hi(21, 0, 0, bank[4])
            act.wait_ge(S["y_done"], STEPS - 1)
            x_hi(22, 0, 1, bank[5])
            h_hi(18, last=True)

            def down_hi(c):
                act.wait_ge(down_landed[c % 4], 16 * (c // 4 + 1))
                act.activation(down_w(c, 0), rows[:, down_slot(c), :], ACT.Copy).then_inc(S["down_hi"], 1)

            def chunk(b, c):
                n = STEPS + IC * b + c
                act.wait_ge(S["z_done"], n + 1)
                act.wait_ge(S["hlo_ready"], n)
                act.activation(sh[:, :], g_ps[:, :], ACT.Silu, scale=gs[:, 0, c:c + 1])\
                   .then_inc(S["silu_ready"], 1)
                for i, part in enumerate(halves(b, c)):
                    act.wait_ge(S["h_ready"], n + 1 + i)
                    act.activation(hslot(c)[:, 0, part], sh[:, part], ACT.Copy)\
                       .then_inc(S["hhi_ready"], 1)

            def mlp_block(b, first=False, last=False):
                for c in range(IC):
                    chunk(b, c)
                    if first:
                        for d in range(3 * c, min(3 * c + 3, IC)):
                            down_hi(d)
                    if c - 1 in PREP_AT and not last:
                        t = PREP_AT[c - 1]
                        x_hi(STEPS + BLOCK * (b + 1) + t, b + 1, (t + 2) % BLOCK)

            mlp_block(0, first=True)
            with act.Fori(1, BLOCKS - 1) as b:
                mlp_block(b)
            mlp_block(BLOCKS - 1, last=True)

        @block.vector
        def _(dve):
            steps = [0]

            def then(ins):
                steps[0] += 1
                ins.then_inc(S["route_step"], 1)
                dve.wait_ge(S["route_step"], steps[0])

            dve.memset(at_least[:, 0, :], 1.0)
            dve.memset(at_least[:, EXPERTS, :], 0.0)
            dve.memset(ones_f[:, :], 1.0)
            dve.wait_ge(S["ids_in"], 16)
            then(dve.tensor_copy(ids_f[:, :], ids_i[:, :]))
            for e in range(1, EXPERTS):
                ins = dve.tensor_scalar(at_least[:, e, :], ids_f[:, :], float(PER_EXPERT * e), None,
                                        ALU.is_ge)
            then(ins)
            then(dve.tensor_tensor(of[:, :, :], at_least[:, 0:EXPERTS, :], at_least[:, 1:EXPERTS + 1, :],
                                   ALU.subtract))
            dve.tensor_tensor_scan(seen[:, :, :].rearrange("p e c -> p (e c)"), ones_f[:, :],
                                   of[:, :, :].rearrange("p e c -> p (e c)"), 0.0, ALU.mult, ALU.add)
            then(dve.tensor_reduce(here[:, :], of[:, :, :], AX, ALU.add))
            dve.tensor_copy(here16[:, :], here[:, :]).then_inc(S["route_sb"], 1)
            dve.wait_ge(S["route_pe"], 1)
            then(dve.tensor_copy(before[:, :, :].rearrange("p a e -> p (a e)"), bank[2][:, 0:2 * EXPERTS]))
            then(dve.tensor_scalar(pad_i[:, :], before[:, 1, :], float(P - 1), None, ALU.add))
            then(dve.tensor_scalar(pad_i[:, :], pad_i[:, :], -P, None, ALU.bitwise_and))
            then(dve.tensor_copy(pad[:, :], pad_i[:, :]))
            dve.tensor_tensor_scan(pad_end[:, :], ones_f[:, 0:EXPERTS], pad[:, :], 0.0, ALU.mult, ALU.add)
            then(dve.tensor_tensor_scan(end[:, :], ones_f[:, 0:EXPERTS], before[:, 1, :], 0.0,
                                        ALU.mult, ALU.add))
            pad_start, start, offset, prior, first, gap = small
            dve.tensor_tensor(pad_start[:, :], pad_end[:, :], pad[:, :], ALU.subtract)
            dve.tensor_tensor(start[:, :], end[:, :], before[:, 1, :], ALU.subtract)
            then(dve.tensor_tensor(prior[:, :], seen[:, :, CT - 1], here[:, :], ALU.subtract))
            dve.tensor_tensor(gap[:, :], pad_start[:, :], start[:, :], ALU.subtract)
            then(dve.tensor_tensor(offset[:, :], before[:, 0, :], pad_start[:, :], ALU.add))
            then(dve.scalar_tensor_tensor(out=first[:, :], in0=offset[:, :], scalar=-1.0,
                                          in1=prior[:, :], op0=ALU.add, op1=ALU.subtract))

            def by_token(a):
                return a[:, :].unsqueeze(2).to_broadcast([P, EXPERTS, CT])

            then(dve.tensor_tensor(pos[0][:, :, :], seen[:, :, :], by_token(first), ALU.add))
            dve.tensor_tensor(pos[1][:, :, :], pos[0][:, :, :], of[:, :, :], ALU.mult)
            then(dve.tensor_tensor(pos[2][:, :, :], of[:, :, :], by_token(gap), ALU.mult))
            dve.tensor_reduce(slot[:, :], pos[1][:, :, :].rearrange("p e c -> p c e"), AX, ALU.add)
            then(dve.tensor_reduce(shift[:, :], pos[2][:, :, :].rearrange("p e c -> p c e"), AX, ALU.add))
            dve.tensor_copy(place_i[:, 0, :], slot[:, :])
            then(dve.tensor_tensor(rank[:, :], slot[:, :], shift[:, :], ALU.subtract))
            then(dve.tensor_copy(place_i[:, 1, :], rank[:, :]))
            dve.tensor_scalar(low_i[:, :, :], place_i[:, :, :], P - 1, None, ALU.bitwise_and)
            then(dve.tensor_scalar(high_i[:, :, :], place_i[:, :, :], 7, None, ALU.logical_shift_right))
            dve.tensor_copy(low[:, :, :], low_i[:, :, :])
            then(dve.tensor_copy(high[:, :, :], high_i[:, :, :]))

            dve.wait_ge(S["consts"], 10)

            def per(a, n):
                return a.unsqueeze(2).to_broadcast([P, CT, n])

            def across(n):
                return iota_p[:, 0:n].unsqueeze(1).to_broadcast([P, CT, n])

            then(dve.tensor_tensor(is_high[:, :, 0, :], per(high[:, 0, :], STEPS), across(STEPS),
                                   ALU.is_equal))
            dve.tensor_tensor(is_high[:, :, 1, :], is_high[:, :, 0, :], per(token[:, :], STEPS), ALU.mult)
            dve.tensor_tensor(is_high[:, :, 2, :], is_high[:, :, 0, :], per(rank[:, :], STEPS), ALU.mult)
            for c in (slice(0, CT // 2), slice(CT // 2, CT)):
                dve.tensor_tensor(is_low[0][:, c, :], per(low[:, 0, :], P)[:, c, :], across(P)[:, c, :],
                                  ALU.is_equal).then_inc(S["route_sb"], 1)
            dve.tensor_scalar(owner[:, 0, :], tile_at[:, :], pad_end[0:1, 0:1], None, ALU.is_ge)
            then(dve.tensor_scalar(owner[:, 1, :], tile_at[:, :], pad_end[0:1, 1:2], None, ALU.is_ge))
            then(dve.tensor_tensor(owner[:, 0, :], owner[:, 0, :], owner[:, 1, :], ALU.add))
            then(dve.scalar_tensor_tensor(out=owner[:, 2, :], in0=tile_at[:, :],
                                          scalar=pad_end[0:1, 2:3], in1=owner[:, 0, :],
                                          op0=ALU.is_ge, op1=ALU.add))
            dve.wait_ge(S["route_pe"], 2)
            dve.tensor_copy(gidx[:, :], bank[3][:, STEPS:2 * STEPS]).then_inc(S["tables_ready"], 1)
            dve.tensor_scalar(owner[:, 3, :], tile_at[:, :], pad_end[0:1, 3:4], None, ALU.is_ge)
            then(dve.tensor_copy(table[:, :, :].rearrange("p a k -> p (a k)"), bank[3][:, 0:3 * STEPS]))
            dve.tensor_copy(tiles[:, :, :], owner[:, 2:4, :])
            then(dve.tensor_scalar(empty[:, 0, :], table[:, 0, :], -1.0, 1.0, ALU.mult, ALU.add))
            for i in range(2):
                dve.tensor_tensor(shifted[:, i, :], tiles[:, 0, 1 - i:1 - i + PACKED], shifts[:, :],
                                  ALU.logical_shift_left)
            then(dve.tensor_tensor(empty[:, 1, :], empty[:, 0, :], dump[:, :], ALU.mult))
            dve.tensor_tensor(sidx[:, :], empty[:, 1, :], table[:, 2, :], ALU.add)\
               .then_inc(S["tables_ready"], 1)
            dve.tensor_reduce(packed[:, :], shifted[:, :, :], AX, ALU.bitwise_xor)\
               .then_inc(S["tables_ready"], 1)
            dve.tensor_tensor(is_low[1][:, :, :], per(low[:, 1, :], P), across(P), ALU.is_equal)
            dve.tensor_tensor(is_high2[:, :, :], per(high[:, 1, :], TILES), across(TILES), ALU.is_equal)\
               .then_inc(S["route_step"], 1)

            def stats(m, at):
                dve.bn_stats(bn[:, 0, :], rows[:, ds(at, 1), :]).then_inc(S["bn_parts"], 1)
                dve.wait_ge(S["bn_parts"], m + 1)
                hold(dve)
                dve.bn_aggr(mv[:, 0, :], bn[:, 0, :]).then_inc(S["bn_mv"], 1)
                dve.wait_ge(S["bn_mv"], m + 1)
                dve.tensor_scalar(ve[:, 0:1], mv[:, 0, 1:2], EPS, None, ALU.add)\
                   .then_inc(S["var_ready"], 1)

            def norm(m, at):
                dve.wait_ge(S["rstd_ready"], m + 1)
                dve.wait_ge(S["xt_done"], m) if not isinstance(m, int) or m else None
                dve.tensor_scalar(xn[:, :], rows[:, ds(at, 1), :], mv[:, 0, 0:1], rstd[:, 0:1],
                                  ALU.subtract, ALU.mult).then_inc(S["xn_ready"], 1)

            def first_stats(t):
                m = STEPS + t
                for i in range(2):
                    dve.bn_stats(bn[:, i, :], rows[:, row_slot(0, t + i), :]).then_inc(S["bn_parts"], 1)
                for i in range(2):
                    dve.wait_ge(S["bn_parts"], m + i + 1)
                    dve.bn_aggr(mv[:, 1 + t + i, :], bn[:, i, :]).then_inc(S["bn_mv"], 1)
                dve.wait_ge(S["bn_mv"], m + 2)
                dve.tensor_scalar(ve[:, 1 + t:3 + t], mv[:, 1 + t:3 + t, 1], EPS, None, ALU.add)\
                   .then_inc(S["var_ready"], 2)

            def first_norm(t):
                m = STEPS + t
                dve.wait_ge(S["rstd_ready"], m + 1)
                if t:
                    dve.wait_ge(S["xt_done"], m - 1)
                dve.tensor_scalar((tmp, xn)[t % 2][:, :], rows[:, row_slot(0, t), :],
                                  mv[:, 1 + t, 0:1], rstd[:, 1 + t:2 + t],
                                  ALU.subtract, ALU.mult).then_inc(S["xn_ready"], 1)

            def x_lo(m, b, u, turned=xt_ps):
                dve.wait_ge(S["xhi_ready"], m + 1)
                dve.tensor_tensor(xpart(b, u, 1), turned[:, :], xpart(b, u, 0).bitcast(F32), ALU.subtract)\
                   .then_inc(S["xlo_ready"], 1)

            def landed(k):
                dve.wait_ge(S["x_landed"], 16 * (k + 1))

            def hidden(k):
                dve.wait_ge(S["silu_ready"], k + 1)
                dve.tensor_tensor(sh[:, :], z_ps[:, :], sh[:, :], ALU.mult).then_inc(S["h_ready"], 1)

            def h_lo(k, last=False):
                dve.wait_ge(S["hhi_ready"], k + 1)
                dve.tensor_tensor(hpart(1, last), ht_ps[:, :], hpart(0, last).bitcast(F32), ALU.subtract)\
                   .then_inc(S["hlo_ready"], 1)

            def update(k):
                at = ring_slot(k)
                dve.wait_ge(S["y_done"], k + 1)
                dve.scalar_tensor_tensor(out=rows[:, ds(at, 1), :], in0=y_ps[:, :].unsqueeze(1),
                                         scalar=tg[:, 0:1], in1=rows[:, ds(at, 1), :],
                                         op0=ALU.mult, op1=ALU.add).then_inc(S["rows_ready"], 1)

            def piece_lo(q):
                dve.wait_ge(S["piece_hi"], q + 1)
                at = ds(q % 2 * PIECE, PIECE)
                dve.tensor_tensor(wgu[:, ds(q // 2, 1), 1, at], raw[:, ds(q % RAWS, 1), :],
                                  wgu[:, ds(q // 2, 1), 0, at].bitcast(F32), ALU.subtract)\
                   .then_inc(S["piece_lo"], 1)

            def check(c):
                dve.wait_ge(S["check_landed"], 16 * (c + 1))
                dve.wait_ge(S["bits_done"], c + 1)
                dve.scalar_tensor_tensor(out=low_bits.unsqueeze(1), in0=checked[:, ds(c % 2, 1), :],
                                         scalar=LO_BITS, in1=low_bits.unsqueeze(1),
                                         op0=ALU.bitwise_and, op1=ALU.bitwise_or)\
                   .then_inc(S["bits_done"], 1)

            def step(k):
                h_lo(k - 1)
                norm(k + 1, ring_slot(k + 1))
                landed(k + 2)
                stats(k + 2, ring_slot(k + 2))
                piece_lo(k - 1)
                hidden(k)
                x_lo(k + 1, 0, 0)
                update(k - 1)

            landed(0)
            stats(0, ring_slot(0))
            dve.wait_ge(S["route_step"], steps[0] + 1)
            dve.tensor_tensor(is_high2[:, :, :], is_high2[:, :, :], per(token[:, :], TILES), ALU.mult)\
               .then_inc(S["route_sb"], 1)
            dve.wait_ge(S["ctx_lo"], POOL_LO_NEXT)
            norm(0, ring_slot(0))
            ctx_lo(dve, 7)
            ctx_lo(dve, 8)
            x_lo(0, 0, 0)
            ctx_lo(dve, 9)
            ctx_lo(dve, 10)
            landed(1)
            stats(1, ring_slot(1))
            ctx_lo(dve, 11)
            norm(1, ring_slot(1))
            ctx_lo(dve, 12)
            ctx_lo(dve, 13)
            hidden(0)
            x_lo(1, 0, 0)
            landed(2)
            stats(2, ring_slot(2))
            dve.wait_ge(S["gates_ready"], 1)
            with dve.Fori(1, IC + 1) as k:
                step(k)
                check(k - 1)
            dve.wait_ge(S["route_pe"], 3)
            dve.tensor_copy(oidx[:, :], bank[4][:, 0:TILES]).then_inc(S["oidx_ready"], 1)
            dve.wait_ge(S["bits_done"], IC + 1)
            dve.tensor_reduce(loose[:, 1:2], low_bits, AX, ALU.max).then_inc(S["loose_step"], 1)
            with dve.Fori(IC + 1, PIECES + 1) as k:
                step(k)
            h_lo(16)
            norm(18, ring_slot(18))
            dve.wait_ge(S["rows_a"], 16)
            first_stats(0)
            hidden(17)
            x_lo(18, 0, 0)
            dve.wait_ge(S["loose_step"], 1)
            first_norm(0)
            first_norm(1)
            dve.wait_ge(S["sums_done"], PIECES)
            dve.tensor_reduce(loose[:, 0:1], lo_sums[:, :], AX, ALU.add).then_inc(S["loose_step"], 1)
            update(16)
            dve.wait_ge(S["loose_step"], 2)
            dve.tensor_tensor(loose[:, 2:3], loose[:, 0:1], loose[:, 1:2], ALU.add)\
               .then_inc(S["loose_step"], 1)
            h_lo(17)
            dve.wait_ge(S["loose_step"], 3)
            dve.tensor_scalar(loose[:, 3:4], loose[:, 2:3], 0.0, None, ALU.not_equal)\
               .then_inc(S["loose_ready"], 1)
            x_lo(19, 0, 2, bank[2])
            dve.wait_ge(S["rows_b"], 16)
            first_stats(2)
            x_lo(20, 0, 3, bank[3])
            first_norm(2)
            first_norm(3)
            hidden(18)
            dve.wait_ge(S["loose_counted"], 1)
            dve.tensor_scalar(flag[:, :], ht_ps[0:1, 0:1], 0.0, None, ALU.is_lt)\
               .then_inc(S["flag_ready"], 1)
            x_lo(21, 0, 0, bank[4])
            x_lo(22, 0, 1, bank[5])
            update(17)
            h_lo(18, last=True)
            update(18)

            def down_lo(c):
                dve.wait_ge(S["down_hi"], c + 1)
                dve.tensor_tensor(down_w(c, 1), rows[:, down_slot(c), :], down_w(c, 0).bitcast(F32),
                                  ALU.subtract).then_inc(S["down_lo"], 1)

            def chunk(b, c):
                n = STEPS + IC * b + c
                dve.wait_ge(S["silu_ready"], n + 1)
                dve.wait_ge(S["u_done"], n - STEPS + 1)
                for part in halves(b, c):
                    dve.scalar_tensor_tensor(out=sh[:, part], in0=u_ps[:, part],
                                             scalar=gs[:, 1, c:c + 1], in1=sh[:, part],
                                             op0=ALU.mult, op1=ALU.mult).then_inc(S["h_ready"], 1)
                for i, part in enumerate(halves(b, c)):
                    dve.wait_ge(S["hhi_ready"], n + 1 + i)
                    dve.tensor_tensor(hslot(c)[:, 1, part], sh[:, part],
                                      hslot(c)[:, 0, part].bitcast(F32), ALU.subtract)\
                       .then_inc(S["hlo_ready"], 1)

            def prepare(b, t):
                m = STEPS + BLOCK * b + t
                at = row_slot(b, t)
                if t == 0:
                    dve.wait_ge(S["rows_a"], 16 * (b + 1))
                if t == 2:
                    dve.wait_ge(S["rows_b"], 16 * (b + 1))
                stats(m, at)
                norm(m, at)

            def scale(b, u):
                n = BLOCK * b + u
                buf = (tmp, xn)[u % 2]
                dve.wait_ge(S["acc_done"], n + 1)
                if u >= 2:
                    dve.wait_ge(S["rows_ready"], STEPS + n - 1)
                dve.tensor_tensor(buf[:, :].unsqueeze(1), acc_ps[u][:, :].unsqueeze(1),
                                  dsb[:, :].unsqueeze(1), ALU.mult).then_inc(S["scaled"], 1)

            def add(b, u):
                at = row_slot(b, (u + 2) % BLOCK)
                dve.wait_ge(S["scaled"], BLOCK * (b + 1) + u + 1)
                dve.tensor_tensor(rows[:, ds(at, 1), :], rows[:, ds(at, 1), :],
                                  (tmp, xn)[u % 2][:, :].unsqueeze(1), ALU.add)\
                   .then_inc(S["rows_ready"], 1)

            def finish(b):
                dve.wait_ge(S["dsb_ready"], 1)
                dve.wait_ge(S["rows_ready"], STEPS + BLOCK * b)
                for u in range(0, BLOCK, 2):
                    scale(b, u)
                    scale(b, u + 1)
                    add(b, u)
                    add(b, u + 1)

            def mlp_block(b, first=False, last=False):
                for c in range(IC):
                    chunk(b, c)
                    if first:
                        for d in range(3 * c, min(3 * c + 3, IC)):
                            down_lo(d)
                    if first and c == IC - 1:
                        dve.tensor_scalar(dsb[:, :], dsb[:, :], tg[:, 1:2], None, ALU.mult)\
                           .then_inc(S["dsb_ready"], 1)
                    if c == 0 and not first:
                        dve.wait_ge(S["xt_done"], STEPS + BLOCK * (b + 1))
                        finish(b - 1)
                    if c - 1 in PREP_AT and not last:
                        t = PREP_AT[c - 1]
                        x_lo(STEPS + BLOCK * (b + 1) + t, b + 1, (t + 2) % BLOCK)
                    if c in PREP_AT and not last:
                        if PREP_AT[c] == 0:
                            dve.wait_ge(S["rows_ready"], STEPS + BLOCK * b)
                        prepare(b + 1, PREP_AT[c])

            dve.sem_inc(S["scaled"], BLOCK)
            mlp_block(0, first=True)
            with dve.Fori(1, BLOCKS - 1) as b:
                mlp_block(b)
            mlp_block(BLOCKS - 1, last=True)
            finish(BLOCKS - 1)

        @block.tensor
        def _(pe):
            pe.wait_ge(S["consts"], 9)
            pe.wait_ge(S["route_sb"], 1)
            pe.matmul(bank[2][:, 0:EXPERTS], tri[:, :], here16[:, :], start=True, stop=True)
            pe.matmul(bank[2][:, EXPERTS:2 * EXPERTS], ones16[:, :], here16[:, :], start=True, stop=True)\
              .then_inc(S["route_pe"], 1)
            for c in range(CT):
                if c % (CT // 2) == 0:
                    pe.wait_ge(S["route_sb"], 2 + c // (CT // 2))
                mm = pe.matmul(bank[3][:, 0:3 * STEPS], is_low[0][:, c, :],
                               is_high[:, c, :, :].rearrange("p a k -> p (a k)"),
                               start=c == 0, stop=c == CT - 1)
            mm.then_inc(S["route_pe"], 1)

            def first_turn_x(t):
                pe.wait_ge(S["xn_ready"], STEPS + t + 1)
                for c in range(KC):
                    mm = pe.transpose(bank[2 + t][:, c * P:(c + 1) * P],
                                      (tmp, xn)[t % 2][:, c * P:(c + 1) * P], ident[:, :])
                mm.then_inc(S["xt_done"], 1)

            def turn_x(m):
                pe.wait_ge(S["xn_ready"], m + 1)
                if not isinstance(m, int) or m:
                    pe.wait_ge(S["xlo_ready"], m)
                for c in range(KC):
                    mm = pe.transpose(xt_ps[:, c * P:(c + 1) * P], xn[:, c * P:(c + 1) * P], ident[:, :])
                mm.then_inc(S["xt_done"], 1)

            def expert_product(out_ps, part, e):
                last = len(PASSES) * KC - 1
                for n in range(last + 1):
                    (s, w), c = PASSES[n // KC], n % KC
                    mm = pe.matmul(out_ps[:, :], part(s)[:, c * P:(c + 1) * P], ctx_w(e, c, w),
                                   start=n == 0, stop=n == last)
                return mm

            def expert(k):
                return pe.value_load(tiles[0:1, 0, ds(k, 1)], min_val=0, max_val=EXPERTS - 1)

            def first_product(k, e=None):
                e = expert(k) if e is None else e
                expert_product(z_ps, lambda s: xpart(0, 0, s), e).then_inc(S["z_done"], 1)

            def turn_h(k):
                pe.wait_ge(S["h_ready"], k + 1)
                for c in range(KC):
                    mm = pe.transpose(ht_ps[:, c * P:(c + 1) * P], sh[:, c * P:(c + 1) * P], ident[:, :])
                mm.then_inc(S["ht_done"], 1)

            def second_product(k, tiles_done=1, e=None):
                expert_product(y_ps, lambda s: hpart(s, last=isinstance(k, int) and k == STEPS - 1),
                               expert(k) if e is None else e).then_inc(S["y_done"], tiles_done)

            def before_first(k):
                pe.wait_ge(S["xlo_ready"], k + 1)

            def before_second(k):
                pe.wait_ge(S["hlo_ready"], k + 1)
                if not isinstance(k, int) or k:
                    pe.wait_ge(S["rows_ready"], k)

            pe.wait_ge(S["route_sb"], 4)
            for c in range(CT):
                mm = pe.matmul(bank[4][:, 0:TILES], is_low[1][:, c, :], is_high2[:, c, :],
                               start=c == 0, stop=c == CT - 1)
            mm.then_inc(S["route_pe"], 1)
            pe.wait_ge(S["tables_ready"], 3)
            e_0 = expert(0)
            these, ones_before = [pe.value_load(packed[0:1, i:i + 1], min_val=0, max_val=4 ** PACKED - 1)
                                  for i in range(2)]
            e_0_split = pe.snap(KC * e_0 + KC)
            turn_x(0)
            before_first(0)
            pe.wait_ge(S["ctx_lo"], e_0_split)
            hold(pe)
            first_product(0, e_0)
            turn_x(1)
            turn_h(0)
            pe.wait_ge(S["ctx_lo"], EXPERTS * KC)

            def expert_step(k, e=None, e_before=None):
                before_first(k)
                first_product(k, e)
                turn_x(k + 1)
                before_second(k - 1)
                second_product(k - 1, e=e_before)
                turn_h(k)

            with pe.Fori(1, PACKED + 1) as k:
                by = pe.snap(2 * (k - 1))
                expert_step(k, *(pe.snap((word >> by) & (EXPERTS - 1), min_val=0, max_val=EXPERTS - 1)
                                 for word in (these, ones_before)))
            expert_step(PACKED + 1)
            before_first(17)
            first_product(17)
            turn_x(18)
            before_second(16)
            second_product(16)
            turn_h(17)
            first_turn_x(0)
            first_turn_x(1)
            before_first(18)

            def last_tiles(empty):
                if empty:
                    pe.sem_inc(S["z_done"], 1)
                else:
                    first_product(18)
                before_second(17)
                pe.wait_ge(S["loose_ready"], 1)
                pe.matmul(ht_ps[0:1, 0:1], loose[:, 3:4], half[:, :], start=True, stop=True)\
                  .then_inc(S["loose_counted"], 1)
                second_product(17, 2 if empty else 1, e=e_17)
                first_turn_x(2)
                first_turn_x(3)
                pe.wait_ge(S["flag_ready"], 1)
                turn_h(18)
                if not empty:
                    before_second(18)
                    second_product(18)

            e_17 = expert(17)
            no_18 = pe.value_load(tiles[0:1, 1, STEPS - 1:STEPS], min_val=0, max_val=1)
            with pe.If(no_18 > 0):
                last_tiles(empty=True)
            with pe.Else():
                last_tiles(empty=False)

            def inner_product(out_ps, b, row, c, passes):
                last = len(passes) * KC - 1
                for n in range(last + 1):
                    (w, s), h = passes[n // KC], n % KC
                    moving = xbuf(b).rearrange("p (u s h j) -> p s h u j", u=BLOCK, s=2, h=KC)[:, s, h]
                    mm = pe.matmul(out_ps[:, :], wgu[:, row + h, w, c * P:(c + 1) * P], moving,
                                   start=n == 0, stop=n == last)
                return mm

            def down_product(b, c, passes):
                pe.wait_ge(S["hlo_ready"], STEPS + IC * b + c + 1)
                pe.wait_ge(S["down_lo"], c + 1)
                for u in range(BLOCK):
                    if len(halves(b, c)) == 2 and u == BLOCK // 2:
                        pe.wait_ge(S["hlo_ready"], STEPS + IC * b + c + 2)
                    if c == 0:
                        pe.wait_ge(S["scaled"], BLOCK * b + u + 1)
                    for n, (w, s) in enumerate(passes):
                        mm = pe.matmul(acc_ps[u][:, :], hslot(c)[:, s, u * P:(u + 1) * P],
                                       down_w(c, w), start=c == 0 and n == 0,
                                       stop=c == IC - 1 and n == len(passes) - 1)
                    if c == IC - 1:
                        mm.then_inc(S["acc_done"], 1)

            def second_mlp(passes):
                with pe.Fori(0, BLOCKS) as b:
                    pe.wait_ge(S["xlo_ready"], STEPS + BLOCK * (b + 1))
                    for c in range(IC):
                        n = STEPS + IC * b + c
                        pe.wait_ge(S["silu_ready"], n)
                        inner_product(g_ps, b, 0, c, passes).then_inc(S["z_done"], 1)
                        if c == 0:
                            pe.wait_ge(S["rows_ready"], STEPS)
                        pe.wait_ge(S["h_ready"], n)
                        inner_product(u_ps, b, KC, c, passes).then_inc(S["u_done"], 1)
                        if c - 1 in PREP_AT:
                            with pe.If(b < BLOCKS - 1):
                                turn_x(STEPS + BLOCK * (b + 1) + PREP_AT[c - 1])
                        if c:
                            down_product(b, c - 1, passes)
                        else:
                            with pe.If(b > 0):
                                down_product(b - 1, IC - 1, passes)
                down_product(BLOCKS - 1, IC - 1, passes)

            pe.wait_ge(S["flag_ready"], 1)
            has_lo = pe.value_load(flag[0:1, 0:1], min_val=0, max_val=1)
            with pe.If(has_lo > 0):
                second_mlp([(0, 0), (1, 0), (0, 1)])
            with pe.Else():
                second_mlp([(0, 0), (0, 1)])


def kernel(x, itok_BxS_13_99985, ctx_2048, g_xattn, g_ffn, L0_ffn_gate_w, L0_ffn_up_w,
           L0_ffn_down_w, L0_ffn_gate_s, L0_ffn_up_s, L0_ffn_down_s):
    import numpy as np
    import concourse.bacc as bacc
    from concourse.bass_utils import run_bass_kernel_spmd

    x, ids, ctx, gate, up, down = (np.asarray(a) for a in (
        x, itok_BxS_13_99985, ctx_2048, L0_ffn_gate_w, L0_ffn_up_w, L0_ffn_down_w))
    arrays = {
        "x": np.ascontiguousarray(x.reshape(TOKENS, D)),
        "ids": np.ascontiguousarray(ids.reshape(P, CT)),
        "ctxT": np.ascontiguousarray(ctx.transpose(0, 2, 1)),
        "g_x": np.asarray(g_xattn),
        "g_f": np.asarray(g_ffn),
        "guT": np.ascontiguousarray(np.concatenate([gate.T, up.T])),
        "dwT": np.ascontiguousarray(down.T),
        "gate_s": np.ascontiguousarray(np.asarray(L0_ffn_gate_s).reshape(IC, P).T),
        "up_s": np.ascontiguousarray(np.asarray(L0_ffn_up_s).reshape(IC, P).T),
        "down_s": np.asarray(L0_ffn_down_s),
    }
    nc = bacc.Bacc("TRN2", target_bir_lowering=False, num_devices=1)
    args = [nc.dram_tensor(n, a.shape, mybir.dt.from_np(a.dtype), kind="ExternalInput").ap()
            for n, a in arrays.items()]
    out = nc.dram_tensor("out", (TOKENS, D), F32, kind="ExternalOutput").ap()
    build(nc, *args, out)
    r = run_bass_kernel_spmd(nc, [arrays], core_ids=[0])
    return r.results[0]["out"].reshape(4, TOKENS // 4, D)
```
